# Optimizing a Trainium2 kernel written in Bass

```python
import numpy as np
import jax
import jax.numpy as jnp

def _softmax(x, axis=-1):
    return jax.nn.softmax(x, axis=axis)

def _gelu(x):
    return jax.nn.gelu(x, approximate=True)

def _silu(x):
    return jax.nn.silu(x)

def _sigmoid(x):
    return jax.nn.sigmoid(x)

def _layernorm(x, axis=-1, eps=1e-05):
    m = jnp.mean(x, axis=axis, keepdims=True)
    v = jnp.var(x, axis=axis, keepdims=True)
    return (x - m) / jnp.sqrt(v + eps)

def _scatter_add(tgt, idx, src, axis=0):
    return tgt.at[idx].add(src)

def _segment_sum(src, seg, n):
    return jax.ops.segment_sum(src, seg, n)
kernel_name = 'mk_sandwich_d1_jaxref_r4_343e3b'

def setup_inputs(seed: int=0):
    np.random.seed(seed)
    _w = jnp.asarray

    def _L0_attn_setup():
        import jax, jax.numpy as jnp
        import numpy as np
        H = 16
        G = 4
        THETA = 10000.0

        def _rope(x, cos, sin):
            x0 = x[..., ::2]
            x1 = x[..., 1::2]
            r0 = x0 * cos - x1 * sin
            r1 = x0 * sin + x1 * cos
            return jnp.stack([r0, r1], axis=-1).reshape(x.shape)
        key = jax.random.key(seed)
        ks = jax.random.split(key, 5)
        B, S, D = (2, 512, 256)
        return {'x': jax.random.normal(ks[0], (B, S, D), jnp.float32), 'Wq': jax.random.normal(ks[1], (D, D), jnp.float32) * 0.02, 'Wk': jax.random.normal(ks[2], (D, D // G), jnp.float32) * 0.02, 'Wv': jax.random.normal(ks[3], (D, D // G), jnp.float32) * 0.02, 'Wo': jax.random.normal(ks[4], (D, D), jnp.float32) * 0.02}
    _L0_attn_in = _L0_attn_setup()

    def _L0_ffn_setup():
        import jax, jax.numpy as jnp
        import numpy as np
        THRESH_FACTOR = 0.7

        def ternary_quantize(w):
            delta = THRESH_FACTOR * jnp.mean(jnp.abs(w))
            return jnp.where(w > delta, 1.0, jnp.where(w < -delta, -1.0, 0.0)).astype(w.dtype)
        key = jax.random.key(seed)
        k1, k2, k3 = jax.random.split(key, 3)
        B, S, D_IN, D_OUT = (8, 1024, 256, 256)
        inp = {'input': jax.random.normal(k1, (B, S, D_IN), dtype=jnp.float32), 'weight': jax.random.normal(k2, (D_OUT, D_IN), dtype=jnp.float32) * (1.0 / np.sqrt(D_IN)), 'alpha': jnp.ones((1,), dtype=jnp.float32), 'bias': jax.random.normal(k3, (D_OUT,), dtype=jnp.float32) * (1.0 / np.sqrt(D_IN))}
        return inp
    _L0_ffn_in = _L0_ffn_setup()
    _d = {'L0_attn_x': _L0_attn_in['x'], 'L0_attn_Wq': _L0_attn_in['Wq'], 'L0_attn_Wk': _L0_attn_in['Wk'], 'L0_attn_Wv': _L0_attn_in['Wv'], 'L0_attn_Wo': _L0_attn_in['Wo'], 'L0_ffn_weight': _L0_ffn_in['weight'], 'L0_ffn_alpha': _L0_ffn_in['alpha'], 'L0_ffn_bias': _L0_ffn_in['bias']}
    _x0 = _d['L0_attn_x']
    _d['L0_attn_x'] = jax.random.normal(jax.random.fold_in(jax.random.key(seed), 1), (8, 1024, 256), dtype=_x0.dtype)
    del _x0
    return _d

def reference(L0_attn_x, L0_attn_Wq, L0_attn_Wk, L0_attn_Wv, L0_attn_Wo, L0_ffn_weight, L0_ffn_alpha, L0_ffn_bias):

    def _L0_attn_ref(x, Wq, Wk, Wv, Wo):
        import jax, jax.numpy as jnp
        import numpy as np
        H = 16
        G = 4
        THETA = 10000.0

        def _rope(x, cos, sin):
            x0 = x[..., ::2]
            x1 = x[..., 1::2]
            r0 = x0 * cos - x1 * sin
            r1 = x0 * sin + x1 * cos
            return jnp.stack([r0, r1], axis=-1).reshape(x.shape)
        B, S, D = x.shape
        hd = D // H
        Hkv = H // G
        q = x @ Wq
        k = x @ Wk
        v = x @ Wv
        k = jnp.repeat(k.reshape(B, S, Hkv, hd), G, axis=2)
        v = jnp.repeat(v.reshape(B, S, Hkv, hd), G, axis=2)
        inv = 1.0 / THETA ** (jnp.arange(0, D, 2, dtype=jnp.float32) / D)
        ang = jnp.arange(S, dtype=jnp.float32)[:, None] * inv[None, :]
        q = _rope(q, jnp.cos(ang)[None], jnp.sin(ang)[None])
        angk = ang[:, :hd // 2]
        k = _rope(k, jnp.cos(angk)[None, :, None, :], jnp.sin(angk)[None, :, None, :])
        q = q.reshape(B, S, H, hd).transpose(0, 2, 1, 3)
        k = k.transpose(0, 2, 1, 3)
        v = v.transpose(0, 2, 1, 3)
        scores = jnp.einsum('bhqd,bhkd->bhqk', q, k) / jnp.sqrt(jnp.float32(D))
        p = jax.nn.softmax(scores, axis=-1)
        o = jnp.einsum('bhqk,bhkd->bhqd', p, v)
        o = o.transpose(0, 2, 1, 3).reshape(B, S, D)
        return o @ Wo

    def _L0_ffn_ref(input, weight, alpha, bias):
        import jax, jax.numpy as jnp
        import numpy as np
        THRESH_FACTOR = 0.7

        def ternary_quantize(w):
            delta = THRESH_FACTOR * jnp.mean(jnp.abs(w))
            return jnp.where(w > delta, 1.0, jnp.where(w < -delta, -1.0, 0.0)).astype(w.dtype)
        w_ternary = ternary_quantize(weight)
        w_eff = w_ternary * alpha
        out = jnp.einsum('bsd,od->bso', input, w_eff) + bias
        return out
    x = L0_attn_x
    x = x + _layernorm(_L0_attn_ref(_layernorm(x, axis=-1), L0_attn_Wq, L0_attn_Wk, L0_attn_Wv, L0_attn_Wo), axis=-1)
    x = x + _layernorm(_L0_ffn_ref(_layernorm(x, axis=-1), L0_ffn_weight, L0_ffn_alpha, L0_ffn_bias), axis=-1)
    return x

_drawn_inputs = setup_inputs


def setup_inputs(seed=0):
    import zlib

    import numpy as np

    out = dict(_drawn_inputs(seed))
    spreads = {}
    factors = {'L0_attn_Wq': 3.738, 'L0_attn_Wk': 3.697, 'L0_ffn_bias': 8.0}
    for name, (base, spread) in spreads.items():
        noise = np.random.default_rng([zlib.crc32(name.encode()), seed]).standard_normal(out[name].shape)
        drawn = base * np.exp(spread * noise) if base else spread * noise
        out[name] = jnp.asarray(drawn.astype(out[name].dtype))
    for name, factor in factors.items():
        out[name] = (out[name] * factor).astype(out[name].dtype)
    return out
```

```python
import concourse.bass as bass
from concourse import mybir
from contextlib import ExitStack

F32 = mybir.dt.float32
BF16 = mybir.dt.bfloat16
ALU = mybir.AluOpType
ACT = mybir.ActivationFunctionType
AX = mybir.AxisListType

P = 128
B, S, D = 8, 1024, 256
H, HKV = 16, 4
G = H // HKV
HD = D // H
NPAIR = HD // 2
HALF = S // 2
KT = S // P
ST = HALF // P
DT = D // P
EPS = 1e-5
THETA = 10000.0
SCALE = float(D) ** -0.5
THRESH = 0.7

QPARTS = (0, 0, 1, 1, 0, 2)
KPARTS = (0, 1, 0, 1, 2, 0)
NBLK = len(QPARTS)
KROWS = NBLK * HD
MROWS = 2
RING = 3
PSLOTS = 4
LAG = 2
AHEAD = 2
STEPS = HKV * KT
LAST = B - 1
NGROUP = 2 * HKV
VCOLS = 32

PRO = {4: [("XT", 0, 0), ("XT", 1, 0)], 5: [("XT", 0, 1), ("XT", 1, 1)],
       6: [("K", 0, 0), ("K", 0, 1)], 7: [("V",)], 9: [("K", 1, 0), ("K", 1, 1)],
       14: [("Q", 0, 0), ("Q", 0, 1)], 18: [("Q", 1, 0), ("Q", 1, 1)]}
EPI = {4: [("OT", 3)], 7: [("ONT", 0), ("ONT", 1)], 8: [("WO", 0), ("WO", 1)],
       19: [("HT", 0), ("HT", 1)], 20: [("FF", 0), ("FF", 1)]}
OWN = {12: [("OT", 0)], 20: [("OT", 1)], 28: [("OT", 2)]}
PRO_JOBS = sum(len(v) for v in PRO.values())
ROPE_STEP = {8: 0, 11: 1, 16: 2, 20: 3}
SPLIT_STEP = {12: 0, 15: 1, 20: 2, 24: 3}


class Half:

    def __init__(self, b, qc, scores=True, maxima=HKV, pro=None, epi=None, base=0, steps=STEPS,
                 load_x=None, flush=True, turn=True):
        self.b, self.qc = b, qc
        self.scores = scores
        self.maxima = maxima
        self.pro = pro
        self.epi = epi
        self.base = base
        self.steps = steps
        self.load_x = load_x
        self.flush = flush
        self.group0 = b * NGROUP + qc * HKV
        self.turn = turn
        self.place = {}
        n = 0
        for s in range(steps):
            if scores:
                for j in range(G):
                    self.place["ST", s, j] = n
                    n += 1
            for job in self.jobs(s):
                self.place[job] = n
                n += 1
        self.count = n

    def turns(self, s):
        if s % KT != 2:
            return False
        g = s // KT
        return self.turn if g == 0 else g <= self.maxima

    def jobs(self, s):
        out = [("MT", s // KT)] if self.turns(s) else []
        if self.pro is not None:
            out += PRO.get(s, [])
        if self.epi is not None:
            out += EPI.get(s, [])
        if self.scores:
            out += OWN.get(s, [])
        return out

    def done(self, *job):
        return self.base + self.place[job] + 1


def sandwich_kernel(nc, x, wq, wk, wv, wo, wf, alpha, bias, rope_q, rope_k, out):
    ctx = ExitStack()
    with ctx:
        def sb(name, shape, dt):
            return ctx.enter_context(nc.sbuf_tensor(name, shape, dt))

        def sem(name):
            return ctx.enter_context(nc.semaphore(name))

        q_rows = sb("q_rows", [KROWS + MROWS, 2, H, HALF], BF16)
        k_rows = sb("k_rows", [KROWS + MROWS, HKV, S], BF16)
        k_next = sb("k_next", [KROWS, HKV, S], BF16)
        q_parts = sb("q_parts", [P, 3, 2, 2, HALF], BF16)
        k_parts = sb("k_parts", [NPAIR * HKV, 3, 2, 2, HALF], BF16)
        probs = sb("probs", [P, PSLOTS, G, HALF], F32)
        v_next = sb("v_next", [P, KT, HKV * HD], F32)
        v_cols = sb("v_cols", [P, HKV, KT, VCOLS], F32)
        row_max = sb("row_max", [P, 2, G * ST], F32)
        max_parts = sb("max_parts", [P, 2, MROWS, G * ST], BF16)
        max_rows = sb("max_rows", [MROWS * G * ST, 2, P], BF16)
        x_in = sb("x_in", [P, KT, D], F32)
        xT = sb("xT", [P, DT, S], F32)
        rot_in = sb("rot_in", [P, 2, 2, HALF], F32)
        rot_mul = sb("rot_mul", [P, 4, HALF], F32)
        rot_out = sb("rot_out", [P, 2, HALF], F32)
        cs_q = sb("cs_q", [P, 2, S], F32)
        cs_k = sb("cs_k", [NPAIR * HKV, 2, S], F32)
        heads = sb("heads", [P, 2, HALF], F32)
        turned = sb("turned", [P, 2, ST, P], F32)
        inv_sum = sb("inv_sum", [P, 2, ST, G], F32)
        attn = sb("attn", [P, ST, D], F32)
        actT = sb("actT", [P, DT, HALF], F32)
        act = sb("act", [P, ST, D], F32)
        res = sb("res", [P, ST, D], F32)
        wq_in = sb("wq_in", [P, DT, D], F32)
        wk_in = sb("wk_in", [P, DT, HKV * HD], F32)
        wv_sb = sb("wv_sb", [P, DT, HKV * HD], F32)
        wq_sb = sb("wq_sb", [P, DT, 2, NPAIR, H], F32)
        wk_sb = sb("wk_sb", [P, DT, 2, NPAIR, HKV], F32)
        wo_sb = sb("wo_sb", [P, DT, D], F32)
        wf_in = sb("wf_in", [P, DT, D], F32)
        wf_tern = sb("wf_tern", [P, DT, D], F32)
        wf_neg = sb("wf_neg", [P, DT, D], F32)
        wfT = sb("wfT", [P, DT, D], F32)
        bias_sb = sb("bias_sb", [P, D], F32)
        alpha_sb = sb("alpha_sb", [P, 1], F32)
        abs_sum = sb("abs_sum", [P, 1], F32)
        delta = sb("delta", [P, 2], F32)
        ones = sb("ones", [P, P], F32)
        ident = sb("ident", [P, P], F32)
        ident_h = sb("ident_h", [P, P], BF16)
        m_half = sb("m_half", [P, KT], F32)

        def stats(name, n):
            return (sb(f"{name}_bn", [P, n, 6], F32), sb(f"{name}_mv", [P, n, 2], F32),
                    sb(f"{name}_nm", [P, n], F32), sb(f"{name}_ve", [P, n], F32),
                    sb(f"{name}_rs", [P, n], F32))

        st_x, st_a, st_y, st_f = stats("sx", KT), stats("sa", ST), stats("sy", ST), stats("sf", ST)

        ring = ctx.enter_context(nc.psum_tensor("ring", [P, RING, 512], F32))
        smax = ctx.enter_context(nc.psum_tensor("smax", [P, 2, 2, 512], F32))
        pv = ctx.enter_context(nc.psum_tensor("pv", [P, 512], F32))

        passed = sem("passed")
        w_loaded = sem("w_loaded")
        consts = sem("consts")
        w_prep = sem("w_prep")
        abs_done = sem("abs_done")
        x_loaded = sem("x_loaded")
        res_loaded = sem("res_loaded")
        ring_full = sem("ring_full")
        ring_read = sem("ring_read")
        max_full = sem("max_full")
        max_read = sem("max_read")
        max_split = sem("max_split")
        max_loaded = sem("max_loaded")
        pv_step = sem("pv_step")
        heads_read = sem("heads_read")
        v_ready = sem("v_ready")
        x_mom = sem("x_mom")
        a_mom = sem("a_mom")
        y_mom = sem("y_mom")
        f_mom = sem("f_mom")
        x_norm = sem("x_norm")
        a_norm = sem("a_norm")
        y_norm = sem("y_norm")
        f_norm = sem("f_norm")
        biased = sem("biased")
        rot_step = sem("rot_step")
        parts_step = sem("parts_step")
        q_loaded = [sem("q_loaded0"), sem("q_loaded1")]
        k_staged = sem("k_staged")
        k_loaded = [sem(f"k_loaded{g}") for g in range(HKV)]
        normed = sem("normed")
        stored = sem("stored")

        def schedule(half, eng):
            h = Half(0, 0, scores=False, maxima=0, pro=0, load_x=None, flush=False, turn=False)
            half(h)
            at = h.count
            h = Half(0, 0, scores=False, maxima=AHEAD, base=at, steps=AHEAD * KT, load_x=1,
                     flush=False, turn=False)
            h.group0 = -AHEAD
            half(h)
            at += h.count
            h = Half(0, 0, pro=1, base=at, flush=False)
            half(h)
            at += h.count
            n1 = Half(0, 1, epi=(0, 0)).count
            n0 = Half(0, 0, pro=0, epi=(0, 0)).count
            with eng.Fori(0, B - 2) as b:
                base = b * (n1 + n0) + at
                half(Half(b, 1, epi=(b, 0), base=base, load_x=b + 2))
                half(Half(b + 1, 0, pro=b + 2, epi=(b, 1), base=base + n1))
            at += (B - 2) * (n1 + n0)
            h = Half(B - 2, 1, epi=(B - 2, 0), base=at)
            half(h)
            at += h.count
            h = Half(LAST, 0, epi=(B - 2, 1), base=at)
            half(h)
            at += h.count
            h = Half(LAST, 1, epi=(LAST, 0), maxima=HKV - AHEAD, base=at)
            half(h)
            at += h.count
            h = Half(B, 0, scores=False, maxima=0, epi=(B - 1, 1), base=at, turn=False)
            half(h)

        def at_least(eng, s, value):
            if not isinstance(value, int) or value > 0:
                eng.wait_ge(s, value)

        block = ctx.enter_context(nc.Block())

        @block.sync
        def _(eng):
            eng.dma_start(x_in[:, :, :], x[0, :, :].rearrange("(t p) d -> p t d", p=P)).then_inc(x_loaded, 16)
            for dst, src in ((wf_in, wf), (wq_in, wq), (wk_in, wk), (wv_sb, wv), (wo_sb, wo)):
                eng.dma_start(dst[:, :, :], src.rearrange("(t p) n -> p t n", p=P)).then_inc(w_loaded, 16)
            eng.dma_start(cs_k[:, :, :], rope_k.rearrange("c p s -> p c s")).then_inc(w_loaded, 16)
            eng.dma_start(cs_q[:, :, :], rope_q.rearrange("c p s -> p c s")).then_inc(w_loaded, 16)
            eng.dma_start(bias_sb[:, :], bias.partition_broadcast(P)).then_inc(w_loaded, 16)
            eng.dma_start(alpha_sb[:, :], alpha.partition_broadcast(P)).then_inc(w_loaded, 16)

            def load_q(b, qc):
                eng.wait_ge(parts_step, b * 16 + 4 * (3 + qc))
                for blk, part in enumerate(QPARTS):
                    for eo in range(2):
                        r = blk * HD + eo * NPAIR
                        eng.dma_start(q_rows[r:r + NPAIR, qc, :, :],
                                      q_parts[:, part, eo, qc, :]).then_inc(q_loaded[qc], 16)

            def stage_k(b):
                eng.wait_ge(parts_step, b * 16 + 8)
                for g in range(HKV):
                    at_least(eng, k_loaded[g], b * 16)
                for blk, part in enumerate(KPARTS):
                    for eo in range(2):
                        r = blk * HD + eo * NPAIR
                        eng.dma_start(k_next[r:r + NPAIR, :, :],
                                      k_parts[:, part, eo, :, :].rearrange("p a n -> p (a n)"))\
                           .then_inc(k_staged, 16)

            def take_k(b, g):
                eng.wait_ge(k_staged, (b + 1) * 16 * 2 * NBLK)
                eng.dma_start(k_rows[0:KROWS, g, :], k_next[:, g, :]).then_inc(k_loaded[g], 16)

            def load_res(b, qc):
                at_least(eng, stored, (b * 2 + qc) * 16)
                eng.dma_start(res[:, :, :], x[bass.ds(b, 1), qc * HALF:(qc + 1) * HALF, :]
                              .rearrange("a (t p) d -> p (a t) d", p=P)).then_inc(res_loaded, 16)

            def half(h):
                if h.load_x is not None:
                    eng.wait_ge(ring_full, h.base)
                    eng.sem_inc(passed, 1)
                    eng.dma_start(x_in[:, :, :], x[bass.ds(h.load_x, 1), :, :]
                                  .rearrange("a (t p) d -> p (a t) d", p=P)).then_inc(x_loaded, 16)
                if h.epi is not None:
                    load_res(*h.epi)
                if h.scores or h.flush:
                    eng.wait_ge(ring_full, h.base)
                    eng.sem_inc(passed, 1)
                if h.scores and h.qc == 1 and h.b is not LAST:
                    load_q(h.b + 1, 0)
                if h.scores and h.qc == 0 and h.flush:
                    load_q(h.b, 1)
                    take_k(h.b, HKV - 1)
                for s in range(h.steps):
                    if h.turns(s):
                        par = (h.qc * HKV + s // KT + 1) % 2 if h.scores else 0
                        eng.wait_ge(ring_read, h.done("MT", s // KT))
                        g, qc = ((h.qc * HKV + s // KT + 1) % HKV, (h.qc * HKV + s // KT + 1) // HKV % 2) \
                            if h.scores else (0, 0)
                        eng.dma_start(q_rows[KROWS:KROWS + MROWS, qc, g * G:(g + 1) * G, :],
                                      max_rows[:, par, :]).then_inc(max_loaded, 16)
                    if h.scores and h.qc == 1 and s % KT == 0 and s > 0 and h.b is not LAST:
                        eng.wait_ge(ring_full, h.done("ST", s - 1, G - 1))
                        take_k(h.b + 1, s // KT - 1)
                    if h.pro is not None and s == 17:
                        stage_k(h.pro)
                        if not h.scores:
                            for g in range(HKV):
                                take_k(0, g)
                    if h.epi is not None and s == STEPS - 1:
                        eb, eq = h.epi
                        eng.wait_ge(f_norm, (eb * 2 + eq + 1) * (ST + 2))
                        eng.dma_start(out[bass.ds(eb, 1), eq * HALF:(eq + 1) * HALF, :]
                                      .rearrange("a (t p) d -> p (a t) d", p=P), res[:, :, :])\
                           .then_inc(stored, 16)
                if h.pro is not None and not h.scores:
                    load_q(0, 0)
                    load_q(0, 1)

            schedule(half, eng)
            eng.wait_ge(stored, 2 * B * 16)

        @block.gpsimd
        def _(eng):
            eng.memset(ident[:, :], 0.0).then_inc(consts, 1)
            eng.memset(ident_h[:, :], 0.0).then_inc(consts, 1)
            eng.wait_ge(consts, 2)
            for m in (ident, ident_h):
                eng.affine_select(out=m[:, :], in_=m[:, :], compare_op=ALU.not_equal, fill=1.0, base=0,
                                  pattern=[[-1, P]], channel_multiplier=1).then_inc(consts, 1)
            eng.memset(ones[:, :], 1.0).then_inc(consts, 1)
            eng.memset(m_half[:, :], -0.5).then_inc(consts, 1)
            eng.wait_ge(consts, 6)
            eng.memset(k_rows[KROWS:KROWS + MROWS, :, :], -1.0).then_inc(consts, 1)
            eng.wait_ge(consts, 7)
            eng.memset(v_cols[:, :, :, :], 0.0).then_inc(consts, 1)
            eng.wait_ge(consts, 8)
            eng.memset(v_cols[:, :, :, HD:HD + 1], 1.0).then_inc(consts, 1)
            eng.wait_ge(consts, CONSTS)

            def normalise(dst, src, st, n, mom, norm, nth, per):
                _, _, nm, ve, rs = st
                eng.wait_ge(mom, (nth + 1) * (2 * n + 2))
                eng.tensor_tensor(rs[:, :], ve[:, :], m_half[:, 0:n], ALU.pow).then_inc(norm, 1)
                eng.wait_ge(norm, nth * per + 1)
                eng.sem_inc(passed, 1)
                for t in range(n):
                    eng.tensor_scalar(dst[:, t, :], src[:, t, :], nm[:, t:t + 1], rs[:, t:t + 1],
                                      ALU.add, ALU.mult).then_inc(norm, 1)

            def rotate(h, r):
                what, part = ("K", r) if r < 2 else ("Q", r - 2)
                n = NPAIR * (HKV if r < 2 else H)
                cs = (cs_k if r < 2 else cs_q)[0:n, :, part * HALF:(part + 1) * HALF]
                even, odd = rot_in[0:n, r % 2, 0, :], rot_in[0:n, r % 2, 1, :]
                nth = h.pro * 4 + r
                eng.wait_ge(ring_read, h.done(what, part, 1))
                at_least(eng, rot_step, nth * 6)
                eng.tensor_tensor(rot_mul[0:n, 0, :], even, cs[:, 0, :], ALU.mult).then_inc(rot_step, 1)
                eng.tensor_tensor(rot_mul[0:n, 1, :], odd, cs[:, 1, :], ALU.mult).then_inc(rot_step, 1)
                eng.tensor_tensor(rot_mul[0:n, 2, :], even, cs[:, 1, :], ALU.mult).then_inc(rot_step, 1)
                eng.tensor_tensor(rot_mul[0:n, 3, :], odd, cs[:, 0, :], ALU.mult).then_inc(rot_step, 1)
                eng.wait_ge(rot_step, nth * 6 + 4)
                at_least(eng, parts_step, nth * 4)
                eng.tensor_tensor(rot_out[0:n, 0, :], rot_mul[0:n, 0, :], rot_mul[0:n, 1, :],
                                  ALU.subtract).then_inc(rot_step, 1)
                eng.tensor_tensor(rot_out[0:n, 1, :], rot_mul[0:n, 2, :], rot_mul[0:n, 3, :],
                                  ALU.add).then_inc(rot_step, 1)

            def take_v(h, b, g):
                eng.sem_inc(passed, 1)
                eng.tensor_copy(v_cols[:, g, :, 0:HD], v_next[:, :, g * HD:(g + 1) * HD])\
                   .then_inc(v_ready, 1)

            def half(h):
                if h.epi is not None:
                    nth = h.epi[0] * 2 + h.epi[1]
                for s in range(h.steps):
                    if h.scores and h.flush and h.qc == 0 and s == 3:
                        eng.wait_ge(pv_step, h.group0 * KT)
                        take_v(h, h.b, HKV - 1)
                    if h.scores and h.qc == 1 and s % KT == 3 and s > KT and h.b is not LAST:
                        g = s // KT - 1
                        eng.wait_ge(pv_step, (h.group0 + g + 1) * KT)
                        take_v(h, h.b + 1, g)
                    if h.pro is not None and s == 3:
                        normalise(x_in, x_in, st_x, KT, x_mom, x_norm, h.pro, KT + 1)
                    if h.pro is not None and s in ROPE_STEP:
                        rotate(h, ROPE_STEP[s])
                        if ROPE_STEP[s] == 1 and not h.scores:
                            eng.wait_ge(ring_read, h.done("V"))
                            for g in range(HKV):
                                take_v(h, 0, g)
                    if h.epi is not None and s == 12:
                        normalise(act, act, st_a, ST, a_mom, a_norm, nth, ST + 2)
                        eng.wait_ge(a_norm, nth * (ST + 2) + ST + 1)
                        eng.wait_ge(res_loaded, (nth + 1) * 16)
                        eng.tensor_tensor(res[:, :, :], res[:, :, :], act[:, :, :], ALU.add).then_inc(a_norm, 1)
                    if h.epi is not None and s == 17:
                        normalise(act, res, st_y, ST, y_mom, y_norm, nth, ST + 1)
                    if h.epi is not None and s == 23:
                        eng.wait_ge(ring_read, h.done("FF", 1))
                        for t in range(ST):
                            eng.tensor_tensor(act[:, t, :], act[:, t, :], bias_sb[:, :], ALU.add)\
                               .then_inc(biased, 1)
                    if h.epi is not None and s == 27:
                        normalise(act, act, st_f, ST, f_mom, f_norm, nth, ST + 2)
                        eng.wait_ge(f_norm, nth * (ST + 2) + ST + 1)
                        eng.tensor_tensor(res[:, :, :], res[:, :, :], act[:, :, :], ALU.add).then_inc(f_norm, 1)

            eng.wait_ge(w_loaded, 9 * 16)
            schedule(half, eng)

        @block.scalar
        def _(eng):
            eng.wait_ge(w_loaded, 9 * 16)
            eng.activation(wf_neg[:, :, :], wf_in[:, :, :], ACT.Abs, accum_out=abs_sum[:, :]).then_inc(abs_done, 1)
            eng.wait_ge(w_prep, WP_WEIGHTS + 1)
            eng.activation(wfT[:, 0, :], ring[:, 0, 0:D], ACT.Copy).then_inc(abs_done, 1)
            eng.activation(wfT[:, 1, :], ring[:, 0, D:2 * D], ACT.Copy).then_inc(abs_done, 1)

            def move(dst, src):
                eng.activation(dst, src, ACT.Copy).then_inc(ring_read, 1)

            def half(h):
                n = 0
                for s in range(h.steps):
                    if s == LAG and h.flush:
                        read_heads(h, -1)
                    if h.scores and s % KT == LAG and s > LAG:
                        read_heads(h, s // KT - 1)
                    if h.scores:
                        step = h.group0 * KT + s
                        at_least(eng, pv_step, step - PSLOTS + 1)
                        for j in range(G):
                            eng.wait_ge(ring_full, h.done("ST", s, j))
                            eng.activation(probs[:, s % PSLOTS, j, :], ring[:, n % RING, :], ACT.Exp,
                                           scale=SCALE).then_inc(ring_read, 1)
                            n += 1
                    for job in h.jobs(s):
                        kind, a = job[0], job[1:]
                        src = ring[:, n % RING, :]
                        eng.wait_ge(ring_full, h.done(*job))
                        if kind == "MT":
                            par = (h.qc * HKV + a[0] + 1) % 2 if h.scores else 0
                            at_least(eng, max_loaded, (h.group0 + a[0]) * 16)
                            move(max_rows[:, par, :], src[0:MROWS * G * ST, 0:P // 2].bitcast(BF16))
                        elif kind == "XT":
                            move(xT[:, a[0], a[1] * HALF:(a[1] + 1) * HALF], src)
                        elif kind in "KQ":
                            r = a[0] if kind == "K" else 2 + a[0]
                            m = NPAIR * (HKV if kind == "K" else H)
                            at_least(eng, rot_step, (h.pro * 4 + r) * 6 - 8)
                            move(rot_in[0:m, r % 2, a[1], :], src[0:m, :])
                        elif kind == "V":
                            at_least(eng, v_ready, h.pro * HKV)
                            move(v_next[:, :, :].rearrange("p t n -> p (t n)"), src)
                        elif kind == "OT":
                            nth = h.group0 + (a[0] if a[0] < 3 else -1)
                            at_least(eng, normed, (nth - 1) * 2)
                            move(turned[:, a[0] % 2, :, :].rearrange("p t n -> p (t n)"), src)
                        elif kind in ("ONT", "HT"):
                            move(actT[:, a[0], :], src)
                        elif kind == "WO":
                            at_least(eng, f_norm, (h.epi[0] * 2 + h.epi[1]) * (ST + 2))
                            move(act[:, 2 * a[0]:2 * a[0] + 2, :].rearrange("p t n -> p (t n)"), src)
                        elif kind == "FF":
                            move(act[:, 2 * a[0]:2 * a[0] + 2, :].rearrange("p t n -> p (t n)"), src)
                        n += 1

            def read_heads(h, g):
                nth = h.group0 + g
                eng.wait_ge(pv_step, (nth + 1) * KT)
                eng.activation(heads[:, g % 2, :], pv[:, :], ACT.Copy).then_inc(heads_read, 1)

            schedule(half, eng)

        @block.tensor
        def _(eng):
            eng.wait_ge(consts, CONSTS)
            eng.wait_ge(abs_done, 1)
            eng.matmul(ring[:, 1, 0:1], ones[:, :], abs_sum[:, :], start=True, stop=True).then_inc(w_prep, 1)
            eng.wait_ge(w_prep, WP_WEIGHTS)
            for dt in range(DT):
                for ot in range(DT):
                    mm = eng.transpose(ring[:, 0, dt * D + ot * P:dt * D + (ot + 1) * P],
                                       wf_tern[:, ot, dt * P:(dt + 1) * P], ident[:, :])
            mm.then_inc(w_prep, 1)
            eng.wait_ge(abs_done, 3)

            def maxima(h, g, unit):
                nth = h.group0 + g + AHEAD
                at = h.qc * HKV + g + (AHEAD if h.scores else 0)
                qc, kv = at // HKV % 2, at % HKV
                row = nth // NGROUP if isinstance(nth, int) else h.b + (at // NGROUP)
                if unit == 0:
                    eng.wait_ge(q_loaded[qc], (row + 1) * 16 * 2 * NBLK)
                    eng.wait_ge(k_loaded[kv], (row + 1) * 16)
                at_least(eng, max_read, nth * G * ST + unit - 1)
                j, qt = unit // ST, unit % ST
                for c in range(2):
                    mm = eng.matmul(smax[:, unit % 2, c, :],
                                    q_rows[0:KROWS, qc, kv * G + j, qt * P:(qt + 1) * P],
                                    k_rows[0:KROWS, kv, c * 512:(c + 1) * 512], start=True, stop=True)
                mm.then_inc(max_full, 1)

            def values(h, s):
                step = h.group0 * KT + s
                g, kt = s // KT % HKV, s % KT
                if kt == 0:
                    at_least(eng, heads_read, h.group0 + s // KT)
                    if h.qc == 0:
                        eng.wait_ge(v_ready, h.b * HKV + g + 1)
                if s >= 0:
                    eng.wait_ge(ring_read, h.done("ST", s, G - 1))
                else:
                    eng.wait_ge(ring_read, h.base)
                for j in range(G):
                    mm = eng.matmul(pv[j * VCOLS:(j + 1) * VCOLS, :], v_cols[:, g, kt, :],
                                    probs[:, s % PSLOTS, j, :], start=(kt == 0), stop=(kt == KT - 1),
                                    skip_group_check=True)
                mm.then_inc(pv_step, 1)

            def half(h):
                n = 0
                for s in range(h.steps):
                    g, kt = s // KT, s % KT
                    if h.scores and kt == 0:
                        eng.wait_ge(max_loaded, (h.group0 + g + 1) * 16)
                    for j in range(G):
                        if h.scores:
                            at_least(eng, ring_read, h.base + (n - RING + 1 if n >= RING else 0))
                            eng.matmul(ring[:, n % RING, :],
                                       k_rows[:, g, kt * P:(kt + 1) * P],
                                       q_rows[:, h.qc, g * G + j, :], start=True, stop=True)\
                               .then_inc(ring_full, 1)
                            n += 1
                        if j % 2 == 1 and g < h.maxima:
                            maxima(h, g, kt * 2 + j // 2)
                    if (h.scores and s >= LAG) or (h.flush and s < LAG):
                        values(h, s - LAG)
                    for job in h.jobs(s):
                        kind, a = job[0], job[1:]
                        dst = ring[:, n % RING, :]
                        at_least(eng, ring_read, h.base + (n - RING + 1 if n >= RING else 0))
                        if kind == "MT":
                            nth = h.group0 + a[0] + 1
                            par = (h.qc * HKV + a[0] + 1) % 2 if h.scores else 0
                            eng.wait_ge(max_split, (nth + 1) * 2)
                            mm = eng.transpose(dst[0:MROWS * G * ST, 0:P // 2].bitcast(BF16),
                                               max_parts[:, par, :, :].rearrange("p m n -> p (m n)"),
                                               ident_h[:, :])
                        elif kind == "XT":
                            eng.wait_ge(x_norm, (h.pro + 1) * (KT + 1))
                            for t in range(ST):
                                mm = eng.transpose(dst[:, t * P:(t + 1) * P],
                                                   x_in[:, a[1] * ST + t, a[0] * P:(a[0] + 1) * P],
                                                   ident[:, :])
                        elif kind in "KQ":
                            w, m = (wk_sb, NPAIR * HKV) if kind == "K" else (wq_sb, NPAIR * H)
                            eng.wait_ge(ring_read, h.done("XT", 1, 1))
                            for dt in range(DT):
                                mm = eng.matmul(dst[0:m, :], w[:, dt, a[1], :, :].rearrange("p i h -> p (i h)"),
                                                xT[:, dt, a[0] * HALF:(a[0] + 1) * HALF],
                                                start=(dt == 0), stop=(dt == DT - 1))
                        elif kind == "V":
                            for t in range(KT):
                                for dt in range(DT):
                                    mm = eng.matmul(dst[:, t * HKV * HD:(t + 1) * HKV * HD],
                                                    xT[:, dt, t * P:(t + 1) * P], wv_sb[:, dt, :],
                                                    start=(dt == 0), stop=(dt == DT - 1))
                        elif kind == "OT":
                            nth = h.group0 + (a[0] if a[0] < 3 else -1)
                            eng.wait_ge(heads_read, nth + 1)
                            for t in range(ST):
                                mm = eng.transpose(dst[:, t * P:(t + 1) * P],
                                                   heads[:, a[0] % 2, t * P:(t + 1) * P], ident[:, :])
                        elif kind == "ONT":
                            eng.wait_ge(normed, h.group0 * 2)
                            for t in range(ST):
                                mm = eng.transpose(dst[:, t * P:(t + 1) * P],
                                                   attn[:, t, a[0] * P:(a[0] + 1) * P], ident[:, :])
                        elif kind == "HT":
                            eng.wait_ge(y_norm, (h.epi[0] * 2 + h.epi[1] + 1) * (ST + 1))
                            for t in range(ST):
                                mm = eng.transpose(dst[:, t * P:(t + 1) * P],
                                                   act[:, t, a[0] * P:(a[0] + 1) * P], ident[:, :])
                        elif kind in ("WO", "FF"):
                            w = wo_sb if kind == "WO" else wfT
                            eng.wait_ge(ring_read, h.done("ONT" if kind == "WO" else "HT", 1))
                            for t in range(2):
                                for dt in range(DT):
                                    mm = eng.matmul(dst[:, t * D:(t + 1) * D],
                                                    actT[:, dt, (2 * a[0] + t) * P:(2 * a[0] + t + 1) * P],
                                                    w[:, dt, :], start=(dt == 0), stop=(dt == DT - 1))
                        mm.then_inc(ring_full, 1)
                        n += 1

            schedule(half, eng)

        @block.vector
        def _(eng):
            eng.wait_ge(w_loaded, 9 * 16)
            for dt in range(DT):
                for eo in range(2):
                    eng.tensor_copy(wq_sb[:, dt, eo, :, :],
                                    wq_in[:, dt, :].rearrange("p (h i e) -> p e i h", h=H, e=2)[:, eo])\
                       .then_inc(w_prep, 1)
                    eng.tensor_copy(wk_sb[:, dt, eo, :, :],
                                    wk_in[:, dt, :].rearrange("p (h i e) -> p e i h", h=HKV, e=2)[:, eo])\
                       .then_inc(w_prep, 1)
            eng.wait_ge(w_prep, WP_SUM)
            eng.tensor_scalar(delta[:, 0:1], ring[:, 1, 0:1], 1.0 / (D * D), THRESH, ALU.mult, ALU.mult)\
               .then_inc(w_prep, 1)
            eng.wait_ge(w_prep, WP_SUM + 1)
            eng.tensor_scalar(delta[:, 1:2], delta[:, 0:1], -1.0, None, ALU.mult).then_inc(w_prep, 1)
            eng.wait_ge(w_prep, WP_SUM + 2)
            eng.wait_ge(abs_done, 1)
            eng.tensor_scalar(wf_tern[:, :, :], wf_in[:, :, :], delta[:, 0:1], None, ALU.is_gt).then_inc(w_prep, 1)
            eng.tensor_scalar(wf_neg[:, :, :], wf_in[:, :, :], delta[:, 1:2], None, ALU.is_lt).then_inc(w_prep, 1)
            eng.wait_ge(w_prep, WP_SUM + 4)
            eng.tensor_tensor(wf_tern[:, :, :], wf_tern[:, :, :], wf_neg[:, :, :], ALU.subtract).then_inc(w_prep, 1)
            eng.wait_ge(w_prep, WP_SUM + 5)
            eng.tensor_scalar(wf_tern[:, :, :], wf_tern[:, :, :], alpha_sb[:, 0:1], None, ALU.mult)\
               .then_inc(w_prep, 1)
            eng.wait_ge(consts, CONSTS)

            def moments(src, st, n, mom, nth):
                bn, mv, nm, ve, _ = st
                per = 2 * n + 2
                for t in range(n):
                    eng.bn_stats(bn[:, t, :], src[:, t, :]).then_inc(mom, 1)
                eng.wait_ge(mom, nth * per + n)
                eng.sem_inc(passed, 1)
                for t in range(n):
                    eng.bn_aggr(mv[:, t, :], bn[:, t, :]).then_inc(mom, 1)
                eng.wait_ge(mom, nth * per + 2 * n)
                eng.tensor_scalar(nm[:, :], mv[:, :, 0], -1.0, None, ALU.mult).then_inc(mom, 1)
                eng.tensor_scalar(ve[:, :], mv[:, :, 1], EPS, None, ALU.add).then_inc(mom, 1)

            def split(h, r):
                n = NPAIR * (HKV if r < 2 else H)
                dst = (k_parts if r < 2 else q_parts)[0:n]
                at = r % 2
                src = rot_out[0:n, :, :]
                nth = h.pro * 4 + r
                eng.wait_ge(rot_step, (nth + 1) * 6)
                if r < 2:
                    at_least(eng, k_staged, h.pro * 16 * 2 * NBLK)
                else:
                    at_least(eng, q_loaded[at], h.pro * 16 * 2 * NBLK)
                eng.tensor_copy(dst[:, 0, :, at, :], src).then_inc(parts_step, 1)
                eng.wait_ge(parts_step, nth * 4 + 1)
                eng.tensor_tensor(src, src, dst[:, 0, :, at, :], ALU.subtract).then_inc(parts_step, 1)
                eng.wait_ge(parts_step, nth * 4 + 2)
                eng.tensor_copy(dst[:, 1, :, at, :], src).then_inc(parts_step, 1)
                eng.wait_ge(parts_step, nth * 4 + 3)
                eng.tensor_tensor(dst[:, 2, :, at, :], src, dst[:, 1, :, at, :], ALU.subtract)\
                   .then_inc(parts_step, 1)

            def divide(h, g):
                nth = h.group0 + (g if g < 3 else -1)
                eng.wait_ge(ring_read, h.done("OT", g))
                if g == 0 and h.epi is not None:
                    eng.wait_ge(ring_full, h.done("ONT", 1))
                src = turned[:, g % 2, :, :].rearrange("p t (j c) -> p t j c", c=VCOLS)
                inv = inv_sum[:, g % 2, :, :]
                at_least(eng, normed, (nth - 1) * 2)
                eng.reciprocal(inv, src[:, :, :, HD]).then_inc(normed, 1)
                eng.wait_ge(normed, nth * 2 + 1)
                eng.tensor_tensor(attn[:, :, g * G * HD:(g + 1) * G * HD].rearrange("p t (j c) -> p t j c", c=HD),
                                  src[:, :, :, 0:HD], inv.unsqueeze(3).broadcast_to([P, ST, G, HD]),
                                  ALU.mult).then_inc(normed, 1)

            def half(h):
                if h.epi is not None:
                    nth_epi = h.epi[0] * 2 + h.epi[1]
                for s in range(h.steps):
                    g, kt = s // KT, s % KT
                    if g < h.maxima:
                        nth = h.group0 + g + AHEAD
                        par = g % 2
                        if kt == 0:
                            at_least(eng, max_split, (nth - 1) * 2)
                        for unit in (2 * kt, 2 * kt + 1):
                            eng.wait_ge(max_full, nth * G * ST + unit + 1)
                            eng.tensor_reduce(row_max[:, par, unit:unit + 1],
                                              smax[:, unit % 2, :, :].rearrange("p c n -> p (c n)"),
                                              AX.X, ALU.max).then_inc(max_read, 1)
                        if kt == KT - 1:
                            eng.wait_ge(max_read, (nth + 1) * G * ST)
                            if h.scores:
                                eng.wait_ge(ring_full, h.done("MT", g) if h.turns(g * KT + 2) else h.base)
                            m1, m2 = max_parts[:, par, 0, :], max_parts[:, par, 1, :]
                            eng.tensor_copy(m1, row_max[:, par, :]).then_inc(max_split, 1)
                            eng.wait_ge(max_split, nth * 2 + 1)
                            eng.tensor_tensor(m2, row_max[:, par, :], m1, ALU.subtract).then_inc(max_split, 1)
                    if h.pro is not None:
                        if s == 1:
                            eng.wait_ge(x_loaded, (h.pro + 1) * 16)
                            at_least(eng, x_norm, h.pro * (KT + 1))
                            moments(x_in, st_x, KT, x_mom, h.pro)
                        if s in SPLIT_STEP:
                            split(h, SPLIT_STEP[s])
                    if h.epi is not None:
                        if s == 5:
                            divide(h, 3)
                        if s == 10:
                            eng.wait_ge(ring_read, h.done("WO", 1))
                            at_least(eng, a_norm, nth_epi * (ST + 2))
                            moments(act, st_a, ST, a_mom, nth_epi)
                        if s == 15:
                            eng.wait_ge(a_norm, (nth_epi + 1) * (ST + 2))
                            at_least(eng, y_norm, nth_epi * (ST + 1))
                            moments(res, st_y, ST, y_mom, nth_epi)
                        if s == 25:
                            eng.wait_ge(biased, (nth_epi + 1) * ST)
                            at_least(eng, f_norm, nth_epi * (ST + 2))
                            moments(act, st_f, ST, f_mom, nth_epi)
                    if h.scores and s in (13, 21, 29):
                        divide(h, s // KT - 1)

            schedule(half, eng)


CONSTS = 9
WP_SUM = 4 * DT + 1
WP_WEIGHTS = WP_SUM + 6


def rope_tables():
    import numpy as np
    inv = 1.0 / THETA ** (np.arange(0, D, 2, dtype=np.float32) / np.float32(D))
    ang = np.arange(S, dtype=np.float32)[None, :] * inv.astype(np.float32)[:, None]
    cs = np.stack([np.cos(ang), np.sin(ang)]).astype(np.float32)
    q = cs.reshape(2, H, NPAIR, S).transpose(0, 2, 1, 3).reshape(2, P, S)
    k = np.repeat(cs[:, :NPAIR, None, :], HKV, axis=2).reshape(2, NPAIR * HKV, S)
    return np.ascontiguousarray(q), np.ascontiguousarray(k)


_INS = ["L0_attn_x", "L0_attn_Wq", "L0_attn_Wk", "L0_attn_Wv", "L0_attn_Wo", "L0_ffn_weight",
        "L0_ffn_alpha", "L0_ffn_bias"]


def kernel(**inputs):
    import numpy as np
    import concourse.bacc as bacc
    from concourse.bass_utils import run_bass_kernel_spmd as run

    nc = bacc.Bacc("TRN2", target_bir_lowering=False, num_devices=1)
    arrays = {f"in_{n}": np.ascontiguousarray(inputs[n]) for n in _INS}
    arrays["rope_q"], arrays["rope_k"] = rope_tables()
    args = [nc.dram_tensor(n, a.shape, F32, kind="ExternalInput").ap() for n, a in arrays.items()]
    out = nc.dram_tensor("out_0", (B, S, D), F32, kind="ExternalOutput").ap()
    sandwich_kernel(nc, *args, out)
    r = run(nc, [arrays], core_ids=[0])
    return r.results[0]["out_0"]
```

```python
import concourse.bass as bass
from concourse import mybir
from contextlib import ExitStack

F32 = mybir.dt.float32
BF16 = mybir.dt.bfloat16
ALU = mybir.AluOpType
ACT = mybir.ActivationFunctionType
AX = mybir.AxisListType

P = 128
B, S, D = 8, 1024, 256
H, HKV = 16, 4
G = H // HKV
HD = D // H
NPAIR = HD // 2
HALF = S // 2
KT = S // P
ST = HALF // P
DT = D // P
EPS = 1e-5
THETA = 10000.0
SCALE = float(D) ** -0.5
THRESH = 0.7

QPARTS = (0, 0, 1, 1, 0, 2)
KPARTS = (0, 1, 0, 1, 2, 0)
NBLK = len(QPARTS)
KROWS = NBLK * HD
MROWS = 2
RING = 3
PSLOTS = 4
LAG = 2
AHEAD = 2
STEPS = HKV * KT
LAST = B - 1
NGROUP = 2 * HKV
VCOLS = 32

PRO = {11: [("XT", 0, 0), ("XT", 1, 0)], 12: [("XT", 0, 1), ("XT", 1, 1)],
       13: [("K", 0)], 14: [("K", 1)], 15: [("V",)], 17: [("Q", 0, 0)], 18: [("Q", 0, 1)]}
PRO1 = {5: [("Q", 1, 0)], 6: [("Q", 1, 1)]}
EPI = {4: [("OT", 3)], 7: [("ONT", 0), ("ONT", 1)], 8: [("WO", 0)], 9: [("WO", 1)],
       22: [("HT", 0), ("HT", 1)], 23: [("FF", 0)], 24: [("FF", 1)]}
OWN = {12: [("OT", 0)], 20: [("OT", 1)], 28: [("OT", 2)]}
X_MOM, A_MOM, Y_MOM, F_MOM = (1, 1), (10, 1), (17, 2), (27, 2)
X_NORM, A_NORM, Y_NORM, BIAS, F_NORM = 9, 14, 19, 25, 29
K_ROT, Q_ROT, Q1_ROT = 16, 20, 7
K_SPLIT, Q_SPLIT, Q1_SPLIT = 19, 0, 19
Q_LOAD = Q_SPLIT + 7
Q_SPLIT0 = 24
K_STAGE = 23
ROT_OPS = (3, 6, 6)
ROT_ALL = sum(ROT_OPS)
SPLIT_OPS = (4, 6, 6)
SPLIT_ALL = sum(SPLIT_OPS)


class Half:

    def __init__(self, b, qc, scores=True, maxima=HKV, pro=None, pro1=None, epi=None, base=0, steps=STEPS,
                 load_x=None, flush=True, turn=True):
        self.b, self.qc = b, qc
        self.scores = scores
        self.maxima = maxima
        self.pro = pro
        self.pro1 = pro1
        self.epi = epi
        self.base = base
        self.steps = steps
        self.load_x = load_x
        self.flush = flush
        self.group0 = b * NGROUP + qc * HKV
        self.turn = turn
        self.place = {}
        n = 0
        for s in range(steps):
            if scores:
                for j in range(G):
                    self.place["ST", s, j] = n
                    n += 1
            for job in self.jobs(s):
                self.place[job] = n
                n += 1
        self.count = n

    def turns(self, s):
        if s % KT != 2:
            return False
        g = s // KT
        return self.turn if g == 0 else g <= self.maxima

    def jobs(self, s):
        out = [("MT", s // KT)] if self.turns(s) else []
        if self.pro is not None:
            out += PRO.get(s, [])
        if self.pro1 is not None:
            out += PRO1.get(s, [])
        if self.epi is not None:
            out += EPI.get(s, [])
        if self.scores:
            out += OWN.get(s, [])
        return out

    def done(self, *job):
        return self.base + self.place[job] + 1


def sandwich_kernel(nc, x, wq, wk, wv, wo, wf, alpha, bias, rope_q, rope_k, out):
    ctx = ExitStack()
    with ctx:
        def sb(name, shape, dt):
            return ctx.enter_context(nc.sbuf_tensor(name, shape, dt))

        def sem(name):
            return ctx.enter_context(nc.semaphore(name))

        q_rows = sb("q_rows", [KROWS + MROWS, 2, H, HALF], BF16)
        k_rows = sb("k_rows", [KROWS + MROWS, HKV, S], BF16)
        k_next = sb("k_next", [KROWS, HKV, S], BF16)
        q_parts = sb("q_parts", [P, 3, 2, 2, HALF], BF16)
        k_parts = sb("k_parts", [P, 3, HALF], BF16)
        probs = sb("probs", [P, PSLOTS, G, HALF], F32)
        v_next = sb("v_next", [P, KT, HKV * HD], F32)
        v_cols = sb("v_cols", [P, HKV, KT, VCOLS], F32)
        row_max = sb("row_max", [P, 2, G * ST], F32)
        max_parts = sb("max_parts", [P, 2, MROWS, G * ST], BF16)
        max_rows = sb("max_rows", [MROWS * G * ST, 2, P], BF16)
        x_in = sb("x_in", [P, KT, D], F32)
        xT = sb("xT", [P, DT, S], F32)
        rot_in = sb("rot_in", [P, 2, 2, HALF], F32)
        rot_mul = sb("rot_mul", [P, 4, HALF], F32)
        rot_out = sb("rot_out", [P, 2, HALF], F32)
        cs_q = sb("cs_q", [P, 2, S], F32)
        cs_k = sb("cs_k", [P, 2, HALF], F32)
        heads = sb("heads", [P, 2, HALF], F32)
        turned = sb("turned", [P, 2, ST, P], F32)
        inv_sum = sb("inv_sum", [P, 2, ST, G], F32)
        attn = sb("attn", [P, ST, D], F32)
        actT = sb("actT", [P, DT, HALF], F32)
        act = sb("act", [P, ST, D], F32)
        res = sb("res", [P, ST, D], F32)
        wq_in = sb("wq_in", [P, DT, D], F32)
        wk_in = sb("wk_in", [P, DT, HKV * HD], F32)
        wv_sb = sb("wv_sb", [P, DT, HKV * HD], F32)
        wq_sb = sb("wq_sb", [P, DT, 2, NPAIR, H], F32)
        wk_sb = sb("wk_sb", [P, DT, 2, NPAIR, HKV], F32)
        wo_sb = sb("wo_sb", [P, DT, D], F32)
        wf_in = sb("wf_in", [P, DT, D], F32)
        wf_tern = sb("wf_tern", [P, DT, D], F32)
        wf_neg = sb("wf_neg", [P, DT, D], F32)
        wfT = sb("wfT", [P, DT, D], F32)
        bias_sb = sb("bias_sb", [P, D], F32)
        alpha_sb = sb("alpha_sb", [P, 1], F32)
        abs_sum = sb("abs_sum", [P, 1], F32)
        delta = sb("delta", [P, 2], F32)
        ones = sb("ones", [P, P], F32)
        ident = sb("ident", [P, P], F32)
        ident_h = sb("ident_h", [P, P], BF16)
        m_half = sb("m_half", [P, KT], F32)

        def stats(name, n):
            return (sb(f"{name}_bn", [P, n, 6], F32), sb(f"{name}_mv", [P, n, 2], F32),
                    sb(f"{name}_nm", [P, n], F32), sb(f"{name}_ve", [P, n], F32),
                    sb(f"{name}_rs", [P, n], F32))

        st_x, st_a, st_y, st_f = stats("sx", KT), stats("sa", ST), stats("sy", ST), stats("sf", ST)

        ring = ctx.enter_context(nc.psum_tensor("ring", [P, RING, 512], F32))
        smax = ctx.enter_context(nc.psum_tensor("smax", [P, 2, 2, 512], F32))
        pv = ctx.enter_context(nc.psum_tensor("pv", [P, 512], F32))

        passed = sem("passed")
        proj_loaded = sem("proj_loaded")
        late_loaded = sem("late_loaded")
        consts = sem("consts")
        w_cols = sem("w_cols")
        w_prep = sem("w_prep")
        abs_done = sem("abs_done")
        x_loaded = sem("x_loaded")
        res_loaded = sem("res_loaded")
        ring_full = sem("ring_full")
        ring_read = sem("ring_read")
        max_full = sem("max_full")
        max_read = sem("max_read")
        max_split = sem("max_split")
        max_loaded = sem("max_loaded")
        pv_step = sem("pv_step")
        heads_read = sem("heads_read")
        v_ready = sem("v_ready")
        x_mom = sem("x_mom")
        a_mom = sem("a_mom")
        y_mom = sem("y_mom")
        f_mom = sem("f_mom")
        x_norm = sem("x_norm")
        a_norm = sem("a_norm")
        y_norm = sem("y_norm")
        f_norm = sem("f_norm")
        biased = sem("biased")
        rot_step = sem("rot_step")
        parts_step = sem("parts_step")
        q_loaded = [sem("q_loaded0"), sem("q_loaded1")]
        k_staged = sem("k_staged")
        k_loaded = [sem(f"k_loaded{g}") for g in range(HKV)]
        normed = sem("normed")
        stored = sem("stored")

        def schedule(half, eng, prepare=None):
            h = Half(0, 0, scores=False, maxima=0, pro=0, load_x=None, flush=False, turn=False)
            half(h)
            at = h.count
            if prepare:
                prepare(at)
            h = Half(0, 0, scores=False, maxima=AHEAD, base=at, steps=AHEAD * KT, load_x=1, pro1=0,
                     flush=False, turn=False)
            h.group0 = -AHEAD
            half(h)
            at += h.count
            h = Half(0, 0, pro=1, base=at, flush=False)
            half(h)
            at += h.count
            n1 = Half(0, 1, pro1=0, epi=(0, 0)).count
            n0 = Half(0, 0, pro=0, epi=(0, 0)).count
            with eng.Fori(0, B - 2) as b:
                base = b * (n1 + n0) + at
                half(Half(b, 1, pro1=b + 1, epi=(b, 0), base=base, load_x=b + 2))
                half(Half(b + 1, 0, pro=b + 2, epi=(b, 1), base=base + n1))
            at += (B - 2) * (n1 + n0)
            h = Half(B - 2, 1, pro1=LAST, epi=(B - 2, 0), base=at)
            half(h)
            at += h.count
            h = Half(LAST, 0, epi=(B - 2, 1), base=at)
            half(h)
            at += h.count
            h = Half(LAST, 1, epi=(LAST, 0), maxima=HKV - AHEAD, base=at)
            half(h)
            at += h.count
            h = Half(B, 0, scores=False, maxima=0, epi=(B - 1, 1), base=at, turn=False)
            half(h)

        def at_least(eng, s, value):
            if not isinstance(value, int) or value > 0:
                eng.wait_ge(s, value)

        block = ctx.enter_context(nc.Block())

        @block.sync
        def _(eng):
            eng.sem_inc(stored, RAISED)
            eng.dma_start(x_in[:, :, :], x[0, :, :].rearrange("(t p) d -> p t d", p=P)).then_inc(x_loaded, 16)
            for dst, src in ((wk_in, wk), (wq_in, wq), (wv_sb, wv)):
                eng.dma_start(dst[:, :, :], src.rearrange("(t p) n -> p t n", p=P)).then_inc(proj_loaded, 16)
            eng.dma_start(cs_k[:, :, :], rope_k).then_inc(proj_loaded, 16)
            eng.dma_start(cs_q[:, :, :], rope_q.rearrange("c p s -> p c s")).then_inc(proj_loaded, 16)
            for dst, src in ((wf_in, wf), (wo_sb, wo)):
                eng.dma_start(dst[:, :, :], src.rearrange("(t p) n -> p t n", p=P)).then_inc(late_loaded, 16)
            eng.dma_start(bias_sb[:, :], bias.partition_broadcast(P)).then_inc(late_loaded, 16)
            eng.dma_start(alpha_sb[:, :], alpha.partition_broadcast(P)).then_inc(late_loaded, 16)

            def load_q(b, qc):
                eng.wait_ge(parts_step, b * SPLIT_ALL + sum(SPLIT_OPS[:2 + qc]))
                for blk, part in enumerate(QPARTS):
                    for eo in range(2):
                        r = blk * HD + eo * NPAIR
                        eng.dma_start(q_rows[r:r + NPAIR, qc, :, :],
                                      q_parts[:, part, eo, qc, :]).then_inc(q_loaded[qc], 16)

            def stage_k(b):
                eng.wait_ge(parts_step, b * SPLIT_ALL + SPLIT_OPS[0])
                for g in range(HKV):
                    at_least(eng, k_loaded[g], b * 16)
                for blk, part in enumerate(KPARTS):
                    for a in range(2):
                        eng.dma_start(k_next[blk * HD:(blk + 1) * HD, :, a * HALF:(a + 1) * HALF],
                                      k_parts[a * P // 2:(a + 1) * P // 2, part, :]).then_inc(k_staged, 16)

            def take_k(b, g):
                eng.wait_ge(k_staged, (b + 1) * 16 * 2 * NBLK)
                eng.dma_start(k_rows[0:KROWS, g, :], k_next[:, g, :]).then_inc(k_loaded[g], 16)

            def load_res(b, qc):
                eng.wait_ge(stored, RAISED + (b * 2 + qc) * 16)
                eng.dma_start(res[:, :, :], x[bass.ds(b, 1), qc * HALF:(qc + 1) * HALF, :]
                              .rearrange("a (t p) d -> p (a t) d", p=P)).then_inc(res_loaded, 16)

            def half(h):
                if h.load_x is not None:
                    eng.wait_ge(ring_full, h.base)
                    eng.sem_inc(passed, 1)
                    eng.dma_start(x_in[:, :, :], x[bass.ds(h.load_x, 1), :, :]
                                  .rearrange("a (t p) d -> p (a t) d", p=P)).then_inc(x_loaded, 16)
                if h.epi is not None:
                    load_res(*h.epi)
                if h.scores or h.flush:
                    eng.wait_ge(ring_full, h.base)
                    eng.sem_inc(passed, 1)
                if h.scores and h.qc == 0 and h.flush:
                    load_q(h.b, 1)
                    take_k(h.b, HKV - 1)
                if h.scores and h.qc == 0 and not h.flush:
                    load_q(0, 1)
                for s in range(h.steps):
                    if s == Q_LOAD and h.scores and h.pro1 is not None:
                        load_q(h.pro1, 0)
                    if h.turns(s):
                        par = (h.qc * HKV + s // KT + 1) % 2 if h.scores else 0
                        eng.wait_ge(ring_read, h.done("MT", s // KT))
                        g, qc = ((h.qc * HKV + s // KT + 1) % HKV, (h.qc * HKV + s // KT + 1) // HKV % 2) \
                            if h.scores else (0, 0)
                        eng.dma_start(q_rows[KROWS:KROWS + MROWS, qc, g * G:(g + 1) * G, :],
                                      max_rows[:, par, :]).then_inc(max_loaded, 16)
                    if h.scores and h.qc == 1 and s % KT == 0 and s > 0 and h.b is not LAST:
                        eng.wait_ge(ring_full, h.done("ST", s - 1, G - 1))
                        take_k(h.b + 1, s // KT - 1)
                    if h.pro is not None and s == K_STAGE:
                        stage_k(h.pro)
                        if not h.scores:
                            for g in range(HKV):
                                take_k(0, g)
                    if h.epi is not None and s == STEPS - 1:
                        eb, eq = h.epi
                        eng.wait_ge(f_norm, RAISED + (eb * 2 + eq + 1) * (ST + 2))
                        eng.dma_start(out[bass.ds(eb, 1), eq * HALF:(eq + 1) * HALF, :]
                                      .rearrange("a (t p) d -> p (a t) d", p=P), res[:, :, :])\
                           .then_inc(stored, 16)
                if h.pro is not None and not h.scores:
                    load_q(0, 0)

            schedule(half, eng)
            eng.wait_ge(stored, RAISED + 2 * B * 16)

        @block.gpsimd
        def _(eng):
            for s in (x_norm, a_norm, y_norm, f_norm):
                eng.sem_inc(s, RAISED)
            eng.memset(ident[:, :], 0.0).then_inc(consts, 1)
            eng.memset(ident_h[:, :], 0.0).then_inc(consts, 1)
            eng.wait_ge(consts, 2)
            for m in (ident, ident_h):
                eng.affine_select(out=m[:, :], in_=m[:, :], compare_op=ALU.not_equal, fill=1.0, base=0,
                                  pattern=[[-1, P]], channel_multiplier=1).then_inc(consts, 1)
            eng.memset(ones[:, :], 1.0).then_inc(consts, 1)
            eng.memset(m_half[:, :], -0.5).then_inc(consts, 1)
            eng.wait_ge(consts, 6)
            eng.memset(k_rows[KROWS:KROWS + MROWS, :, :], -1.0).then_inc(consts, 1)
            eng.wait_ge(consts, 7)
            eng.memset(v_cols[:, :, :, :], 0.0).then_inc(consts, 1)
            eng.wait_ge(consts, 8)
            eng.memset(v_cols[:, :, :, HD:HD + 1], 1.0).then_inc(consts, 1)
            eng.wait_ge(consts, CONSTS)

            def normalise(dst, src, st, n, mom, norm, nth, per):
                _, _, nm, ve, rs = st
                eng.wait_ge(mom, (nth + 1) * (2 * n + 2))
                eng.tensor_tensor(rs[:, :], ve[:, :], m_half[:, 0:n], ALU.pow).then_inc(norm, 1)
                eng.wait_ge(norm, RAISED + nth * per + 1)
                eng.sem_inc(passed, 1)
                for t in range(n):
                    eng.tensor_scalar(dst[:, t, :], src[:, t, :], nm[:, t:t + 1], rs[:, t:t + 1],
                                      ALU.add, ALU.mult).then_inc(norm, 1)

            def rotate_k(h):
                own, other = rot_in[:, 0, 0, :], rot_in[:, 0, 1, :]
                eng.wait_ge(ring_read, h.done("K", 1))
                at_least(eng, rot_step, h.pro * ROT_ALL)
                eng.tensor_tensor(rot_mul[:, 0, :], own, cs_k[:, 0, :], ALU.mult).then_inc(rot_step, 1)
                eng.tensor_tensor(rot_mul[:, 1, :], other, cs_k[:, 1, :], ALU.mult).then_inc(rot_step, 1)
                eng.wait_ge(rot_step, h.pro * ROT_ALL + 2)
                at_least(eng, parts_step, h.pro * SPLIT_ALL)
                eng.tensor_tensor(rot_out[:, 0, :], rot_mul[:, 0, :], rot_mul[:, 1, :],
                                  ALU.add).then_inc(rot_step, 1)

            def rotate_q(h, row, a):
                cs = cs_q[:, :, a * HALF:(a + 1) * HALF]
                even, odd = rot_in[:, 1, 0, :], rot_in[:, 1, 1, :]
                before = row * ROT_ALL + sum(ROT_OPS[:a + 1])
                eng.wait_ge(ring_read, h.done("Q", a, 1))
                eng.wait_ge(rot_step, before)
                eng.tensor_tensor(rot_mul[:, 0, :], even, cs[:, 0, :], ALU.mult).then_inc(rot_step, 1)
                eng.tensor_tensor(rot_mul[:, 1, :], odd, cs[:, 1, :], ALU.mult).then_inc(rot_step, 1)
                eng.tensor_tensor(rot_mul[:, 2, :], even, cs[:, 1, :], ALU.mult).then_inc(rot_step, 1)
                eng.tensor_tensor(rot_mul[:, 3, :], odd, cs[:, 0, :], ALU.mult).then_inc(rot_step, 1)
                eng.wait_ge(rot_step, before + 4)
                eng.wait_ge(parts_step, row * SPLIT_ALL + sum(SPLIT_OPS[:a + 1]))
                eng.tensor_tensor(rot_out[:, 0, :], rot_mul[:, 0, :], rot_mul[:, 1, :],
                                  ALU.subtract).then_inc(rot_step, 1)
                eng.tensor_tensor(rot_out[:, 1, :], rot_mul[:, 2, :], rot_mul[:, 3, :],
                                  ALU.add).then_inc(rot_step, 1)

            def take_v(h, b, g):
                eng.sem_inc(passed, 1)
                eng.tensor_copy(v_cols[:, g, :, 0:HD], v_next[:, :, g * HD:(g + 1) * HD])\
                   .then_inc(v_ready, 1)

            def half(h):
                if h.epi is not None:
                    nth = h.epi[0] * 2 + h.epi[1]
                for s in range(h.steps):
                    if h.scores and h.flush and h.qc == 0 and s == 3:
                        eng.wait_ge(pv_step, h.group0 * KT)
                        take_v(h, h.b, HKV - 1)
                    if h.scores and h.qc == 1 and s % KT == 3 and s > KT and h.b is not LAST:
                        g = s // KT - 1
                        eng.wait_ge(pv_step, (h.group0 + g + 1) * KT)
                        take_v(h, h.b + 1, g)
                    if h.pro is not None and s == X_NORM:
                        normalise(x_in, x_in, st_x, KT, x_mom, x_norm, h.pro, KT + 1)
                    if h.pro is not None and s == K_ROT:
                        rotate_k(h)
                        if not h.scores:
                            eng.wait_ge(ring_read, h.done("V"))
                            for g in range(HKV):
                                take_v(h, 0, g)
                    if h.pro is not None and s == Q_ROT:
                        rotate_q(h, h.pro, 0)
                    if h.pro1 is not None and s == Q1_ROT:
                        rotate_q(h, h.pro1, 1)
                    if h.epi is not None and s == A_NORM:
                        normalise(act, act, st_a, ST, a_mom, a_norm, nth, ST + 2)
                        eng.wait_ge(a_norm, RAISED + nth * (ST + 2) + ST + 1)
                        eng.wait_ge(res_loaded, (nth + 1) * 16)
                        eng.tensor_tensor(res[:, :, :], res[:, :, :], act[:, :, :], ALU.add).then_inc(a_norm, 1)
                    if h.epi is not None and s == Y_NORM:
                        normalise(act, res, st_y, ST, y_mom, y_norm, nth, ST + 1)
                    if h.epi is not None and s == BIAS:
                        eng.wait_ge(ring_read, h.done("FF", 1))
                        for t in range(ST):
                            eng.tensor_tensor(act[:, t, :], act[:, t, :], bias_sb[:, :], ALU.add)\
                               .then_inc(biased, 1)
                    if h.epi is not None and s == F_NORM:
                        normalise(act, act, st_f, ST, f_mom, f_norm, nth, ST + 2)
                        eng.wait_ge(f_norm, RAISED + nth * (ST + 2) + ST + 1)
                        eng.tensor_tensor(res[:, :, :], res[:, :, :], act[:, :, :], ALU.add).then_inc(f_norm, 1)

            eng.wait_ge(proj_loaded, 5 * 16)
            eng.wait_ge(late_loaded, 4 * 16)
            schedule(half, eng)

        @block.scalar
        def _(eng):
            def prepare(at):
                eng.wait_ge(late_loaded, 4 * 16)
                eng.activation(wf_neg[:, :, :], wf_in[:, :, :], ACT.Abs, accum_out=abs_sum[:, :])\
                   .then_inc(abs_done, 1)
                eng.wait_ge(w_prep, WP_TURNED)
                eng.activation(wfT[:, 0, :], ring[:, 0, 0:D], ACT.Copy).then_inc(abs_done, 1)
                eng.activation(wfT[:, 1, :], ring[:, 0, D:2 * D], ACT.Copy).then_inc(abs_done, 1)

            def move(dst, src):
                eng.activation(dst, src, ACT.Copy).then_inc(ring_read, 1)

            def half(h):
                n = 0
                for s in range(h.steps):
                    if s % KT == LAG and ((s > LAG and h.scores) or (s == LAG and h.flush)):
                        read_heads(h, s // KT - 1)
                    if h.scores:
                        step = h.group0 * KT + s
                        at_least(eng, pv_step, step - PSLOTS + 1)
                        for j in range(G):
                            eng.wait_ge(ring_full, h.done("ST", s, j))
                            eng.activation(probs[:, s % PSLOTS, j, :], ring[:, n % RING, :], ACT.Exp,
                                           scale=SCALE).then_inc(ring_read, 1)
                            n += 1
                    for job in h.jobs(s):
                        kind, a = job[0], job[1:]
                        src = ring[:, n % RING, :]
                        eng.wait_ge(ring_full, h.done(*job))
                        if kind == "MT":
                            par = (h.qc * HKV + a[0] + 1) % 2 if h.scores else 0
                            at_least(eng, max_loaded, (h.group0 + a[0]) * 16)
                            move(max_rows[:, par, :], src[0:MROWS * G * ST, 0:P // 2].bitcast(BF16))
                        elif kind == "XT":
                            move(xT[:, a[0], a[1] * HALF:(a[1] + 1) * HALF], src)
                        elif kind == "K":
                            at_least(eng, rot_step, (h.pro - 1) * ROT_ALL + 2)
                            move(rot_in[:, 0, a[0], :], src)
                        elif kind == "Q":
                            row = h.pro1 if a[0] else h.pro
                            at_least(eng, rot_step, row * ROT_ALL + (7 if a[0] else -2))
                            move(rot_in[:, 1, a[1], :], src)
                        elif kind == "V":
                            at_least(eng, v_ready, h.pro * HKV)
                            move(v_next[:, :, :].rearrange("p t n -> p (t n)"), src)
                        elif kind == "OT":
                            nth = h.group0 + (a[0] if a[0] < 3 else -1)
                            at_least(eng, normed, (nth - 1) * 2)
                            move(turned[:, a[0] % 2, :, :].rearrange("p t n -> p (t n)"), src)
                        elif kind in ("ONT", "HT"):
                            move(actT[:, a[0], :], src)
                        elif kind == "WO":
                            eng.wait_ge(f_norm, RAISED + (h.epi[0] * 2 + h.epi[1]) * (ST + 2))
                            move(act[:, 2 * a[0]:2 * a[0] + 2, :].rearrange("p t n -> p (t n)"), src)
                        elif kind == "FF":
                            move(act[:, 2 * a[0]:2 * a[0] + 2, :].rearrange("p t n -> p (t n)"), src)
                        n += 1

            def read_heads(h, g):
                nth = h.group0 + g
                eng.wait_ge(pv_step, (nth + 1) * KT)
                eng.activation(heads[:, g % 2, :], pv[:, :], ACT.Copy).then_inc(heads_read, 1)

            schedule(half, eng, prepare)

        @block.tensor
        def _(eng):
            eng.wait_ge(consts, CONSTS)
            eng.wait_ge(proj_loaded, 5 * 16)
            eng.wait_ge(w_cols, 4 * DT)

            def prepare(at):
                eng.wait_ge(ring_read, at)
                eng.wait_ge(abs_done, 1)
                eng.matmul(ring[:, 1, 0:1], ones[:, :], abs_sum[:, :], start=True, stop=True)\
                   .then_inc(w_prep, 1)
                eng.wait_ge(w_prep, WP_TURNED - 1)
                for dt in range(DT):
                    for ot in range(DT):
                        mm = eng.transpose(ring[:, 0, dt * D + ot * P:dt * D + (ot + 1) * P],
                                           wf_tern[:, ot, dt * P:(dt + 1) * P], ident[:, :])
                mm.then_inc(w_prep, 1)
                eng.wait_ge(abs_done, 3)

            def maxima(h, g, unit):
                nth = h.group0 + g + AHEAD
                at = h.qc * HKV + g + (AHEAD if h.scores else 0)
                qc, kv = at // HKV % 2, at % HKV
                row = nth // NGROUP if isinstance(nth, int) else h.b + (at // NGROUP)
                if unit == 0:
                    eng.wait_ge(q_loaded[qc], (row + 1) * 16 * 2 * NBLK)
                    eng.wait_ge(k_loaded[kv], (row + 1) * 16)
                at_least(eng, max_read, nth * G * ST + unit - 1)
                j, qt = unit // ST, unit % ST
                for c in range(2):
                    mm = eng.matmul(smax[:, unit % 2, c, :],
                                    q_rows[0:KROWS, qc, kv * G + j, qt * P:(qt + 1) * P],
                                    k_rows[0:KROWS, kv, c * 512:(c + 1) * 512], start=True, stop=True)
                mm.then_inc(max_full, 1)

            def values(h, s):
                step = h.group0 * KT + s
                g, kt = s // KT % HKV, s % KT
                if kt == 0:
                    at_least(eng, heads_read, h.group0 + s // KT)
                    if h.qc == 0:
                        eng.wait_ge(v_ready, h.b * HKV + g + 1)
                if s >= 0:
                    eng.wait_ge(ring_read, h.done("ST", s, G - 1))
                else:
                    eng.wait_ge(ring_read, h.base)
                for j in range(G):
                    mm = eng.matmul(pv[j * VCOLS:(j + 1) * VCOLS, :], v_cols[:, g, kt, :],
                                    probs[:, s % PSLOTS, j, :], start=(kt == 0), stop=(kt == KT - 1),
                                    skip_group_check=True)
                mm.then_inc(pv_step, 1)

            def half(h):
                n = 0
                for s in range(h.steps):
                    g, kt = s // KT, s % KT
                    for j in range(G):
                        if j == 0 and h.scores and kt == 0:
                            eng.wait_ge(max_loaded, (h.group0 + g + 1) * 16)
                        if h.scores:
                            at_least(eng, ring_read, h.base + (n - RING + 1 if n >= RING else 0))
                            eng.matmul(ring[:, n % RING, :],
                                       k_rows[:, g, kt * P:(kt + 1) * P],
                                       q_rows[:, h.qc, g * G + j, :], start=True, stop=True)\
                               .then_inc(ring_full, 1)
                            n += 1
                        if j in (0, 2) and g < h.maxima:
                            maxima(h, g, kt * 2 + j // 2)
                    if (h.scores and s >= LAG) or (h.flush and s < LAG):
                        values(h, s - LAG)
                    for job in h.jobs(s):
                        kind, a = job[0], job[1:]
                        dst = ring[:, n % RING, :]
                        at_least(eng, ring_read, h.base + (n - RING + 1 if n >= RING else 0))
                        if kind == "MT":
                            nth = h.group0 + a[0] + 1
                            par = (h.qc * HKV + a[0] + 1) % 2 if h.scores else 0
                            eng.wait_ge(max_split, (nth + 1) * 2)
                            mm = eng.transpose(dst[0:MROWS * G * ST, 0:P // 2].bitcast(BF16),
                                               max_parts[:, par, :, :].rearrange("p m n -> p (m n)"),
                                               ident_h[:, :])
                        elif kind == "XT":
                            eng.wait_ge(x_norm, RAISED + (h.pro + 1) * (KT + 1))
                            for t in range(ST):
                                mm = eng.transpose(dst[:, t * P:(t + 1) * P],
                                                   x_in[:, a[1] * ST + t, a[0] * P:(a[0] + 1) * P],
                                                   ident[:, :])
                        elif kind == "K":
                            eng.wait_ge(ring_read, h.done("XT", 1, 1))
                            for dt in range(DT):
                                for half_of, eo in ((0, 0), (0, 1), (1, 0), (1, 1)):
                                    tile = (half_of * 2 + eo) * NPAIR * HKV
                                    mm = eng.matmul(dst[tile:tile + NPAIR * HKV, :],
                                                    wk_sb[:, dt, eo ^ a[0], :, :].rearrange("p i h -> p (i h)"),
                                                    xT[:, dt, half_of * HALF:(half_of + 1) * HALF],
                                                    start=(dt == 0), stop=(dt == DT - 1),
                                                    skip_group_check=True)
                        elif kind == "Q":
                            for dt in range(DT):
                                mm = eng.matmul(dst, wq_sb[:, dt, a[1], :, :].rearrange("p i h -> p (i h)"),
                                                xT[:, dt, a[0] * HALF:(a[0] + 1) * HALF],
                                                start=(dt == 0), stop=(dt == DT - 1))
                        elif kind == "V":
                            for t in range(KT):
                                for dt in range(DT):
                                    mm = eng.matmul(dst[:, t * HKV * HD:(t + 1) * HKV * HD],
                                                    xT[:, dt, t * P:(t + 1) * P], wv_sb[:, dt, :],
                                                    start=(dt == 0), stop=(dt == DT - 1))
                        elif kind == "OT":
                            nth = h.group0 + (a[0] if a[0] < 3 else -1)
                            eng.wait_ge(heads_read, nth + 1)
                            for t in range(ST):
                                mm = eng.transpose(dst[:, t * P:(t + 1) * P],
                                                   heads[:, a[0] % 2, t * P:(t + 1) * P], ident[:, :])
                        elif kind == "ONT":
                            eng.wait_ge(normed, h.group0 * 2)
                            for t in range(ST):
                                mm = eng.transpose(dst[:, t * P:(t + 1) * P],
                                                   attn[:, t, a[0] * P:(a[0] + 1) * P], ident[:, :])
                        elif kind == "HT":
                            eng.wait_ge(y_norm, RAISED + (h.epi[0] * 2 + h.epi[1] + 1) * (ST + 1))
                            for t in range(ST):
                                mm = eng.transpose(dst[:, t * P:(t + 1) * P],
                                                   act[:, t, a[0] * P:(a[0] + 1) * P], ident[:, :])
                        elif kind in ("WO", "FF"):
                            w = wo_sb if kind == "WO" else wfT
                            eng.wait_ge(ring_read, h.done("ONT" if kind == "WO" else "HT", 1))
                            for t in range(2):
                                for dt in range(DT):
                                    mm = eng.matmul(dst[:, t * D:(t + 1) * D],
                                                    actT[:, dt, (2 * a[0] + t) * P:(2 * a[0] + t + 1) * P],
                                                    w[:, dt, :], start=(dt == 0), stop=(dt == DT - 1))
                        mm.then_inc(ring_full, 1)
                        n += 1

            schedule(half, eng, prepare)

        @block.vector
        def _(eng):
            eng.wait_ge(proj_loaded, 5 * 16)
            for dt in range(DT):
                for eo in range(2):
                    eng.tensor_copy(wq_sb[:, dt, eo, :, :],
                                    wq_in[:, dt, :].rearrange("p (h i e) -> p e i h", h=H, e=2)[:, eo])\
                       .then_inc(w_cols, 1)
                    eng.tensor_copy(wk_sb[:, dt, eo, :, :],
                                    wk_in[:, dt, :].rearrange("p (h i e) -> p e i h", h=HKV, e=2)[:, eo])\
                       .then_inc(w_cols, 1)
            eng.wait_ge(consts, CONSTS)

            def prepare(at):
                eng.wait_ge(late_loaded, 4 * 16)
                eng.wait_ge(w_prep, 1)
                eng.tensor_scalar(delta[:, 0:1], ring[:, 1, 0:1], 1.0 / (D * D), THRESH, ALU.mult, ALU.mult)\
                   .then_inc(w_prep, 1)
                eng.wait_ge(w_prep, 2)
                eng.tensor_scalar(delta[:, 1:2], delta[:, 0:1], -1.0, None, ALU.mult).then_inc(w_prep, 1)
                eng.wait_ge(w_prep, 3)
                eng.tensor_scalar(wf_tern[:, :, :], wf_in[:, :, :], delta[:, 0:1], None, ALU.is_gt)\
                   .then_inc(w_prep, 1)
                eng.tensor_scalar(wf_neg[:, :, :], wf_in[:, :, :], delta[:, 1:2], None, ALU.is_lt)\
                   .then_inc(w_prep, 1)
                eng.wait_ge(w_prep, 5)
                eng.tensor_tensor(wf_tern[:, :, :], wf_tern[:, :, :], wf_neg[:, :, :], ALU.subtract)\
                   .then_inc(w_prep, 1)
                eng.wait_ge(w_prep, 6)
                eng.tensor_scalar(wf_tern[:, :, :], wf_tern[:, :, :], alpha_sb[:, 0:1], None, ALU.mult)\
                   .then_inc(w_prep, 1)

            def moments(src, st, n, mom, nth, t, tiles):
                bn, mv, nm, ve, _ = st
                at = nth * (2 * n + 2)
                for i in range(t, t + tiles):
                    eng.bn_stats(bn[:, i, :], src[:, i, :]).then_inc(mom, 1)
                if t + tiles == n:
                    eng.wait_ge(mom, at + n)
                    eng.sem_inc(passed, 1)
                    for i in range(n):
                        eng.bn_aggr(mv[:, i, :], bn[:, i, :]).then_inc(mom, 1)
                    eng.wait_ge(mom, at + 2 * n)
                    eng.tensor_scalar(nm[:, :], mv[:, :, 0], -1.0, None, ALU.mult).then_inc(mom, 1)
                    eng.tensor_scalar(ve[:, :], mv[:, :, 1], EPS, None, ALU.add).then_inc(mom, 1)

            def split_k(row, i):
                src, dst = rot_out[:, 0, :], [k_parts[:, m, :] for m in range(3)]
                before = row * SPLIT_ALL
                if i == 0:
                    eng.wait_ge(rot_step, row * ROT_ALL + ROT_OPS[0])
                    at_least(eng, k_staged, row * 16 * 2 * NBLK)
                    eng.tensor_copy(dst[0], src).then_inc(parts_step, 1)
                else:
                    eng.wait_ge(parts_step, before + i)
                    if i == 2:
                        eng.tensor_copy(dst[1], src).then_inc(parts_step, 1)
                    else:
                        out_ = src if i == 1 else dst[2]
                        eng.tensor_tensor(out_, src, dst[i // 2], ALU.subtract).then_inc(parts_step, 1)

            def split_q(row, a, i):
                src, dst = rot_out[:, :, :], [q_parts[:, m, :, a, :] for m in range(3)]
                before = row * SPLIT_ALL + sum(SPLIT_OPS[:a + 1])
                if i == 0:
                    eng.wait_ge(rot_step, row * ROT_ALL + sum(ROT_OPS[:a + 2]))
                    at_least(eng, q_loaded[a], row * 16 * 2 * NBLK)
                    eng.tensor_copy(dst[0], src).then_inc(parts_step, 1)
                elif i == 3:
                    eng.wait_ge(parts_step, before + 3)
                    eng.tensor_copy(dst[1], src).then_inc(parts_step, 1)
                else:
                    eo = (i - 1) % 3
                    eng.wait_ge(parts_step, before + i - eo)
                    out_ = src if i < 3 else dst[2]
                    eng.tensor_tensor(out_[:, eo, :], src[:, eo, :], dst[i // 3][:, eo, :], ALU.subtract)\
                       .then_inc(parts_step, 1)

            def due(s, when, n):
                first, tiles = when
                return ((s - first) * tiles, tiles) if first <= s < first + n // tiles else None

            def divide(h, g):
                nth = h.group0 + (g if g < 3 else -1)
                eng.wait_ge(ring_read, h.done("OT", g))
                if g == 0 and h.epi is not None:
                    eng.wait_ge(ring_full, h.done("ONT", 1))
                src = turned[:, g % 2, :, :].rearrange("p t (j c) -> p t j c", c=VCOLS)
                inv = inv_sum[:, g % 2, :, :]
                at_least(eng, normed, (nth - 1) * 2)
                eng.reciprocal(inv, src[:, :, :, HD]).then_inc(normed, 1)
                eng.wait_ge(normed, nth * 2 + 1)
                eng.tensor_tensor(attn[:, :, g * G * HD:(g + 1) * G * HD].rearrange("p t (j c) -> p t j c", c=HD),
                                  src[:, :, :, 0:HD], inv.unsqueeze(3).broadcast_to([P, ST, G, HD]),
                                  ALU.mult).then_inc(normed, 1)

            def reduce_max(h, g, unit):
                eng.wait_ge(max_full, (h.group0 + g + AHEAD) * G * ST + unit + 1)
                eng.tensor_reduce(row_max[:, g % 2, unit:unit + 1],
                                  smax[:, unit % 2, :, :].rearrange("p c n -> p (c n)"),
                                  AX.X, ALU.max).then_inc(max_read, 1)

            def split_max(h, g):
                nth, par = h.group0 + g + AHEAD, g % 2
                eng.wait_ge(max_read, (nth + 1) * G * ST)
                if h.scores:
                    eng.wait_ge(ring_full, h.done("MT", g))
                m1, m2 = max_parts[:, par, 0, :], max_parts[:, par, 1, :]
                eng.tensor_copy(m1, row_max[:, par, :]).then_inc(max_split, 1)
                eng.wait_ge(max_split, nth * 2 + 1)
                eng.tensor_tensor(m2, row_max[:, par, :], m1, ALU.subtract).then_inc(max_split, 1)

            def half(h):
                if h.epi is not None:
                    nth_epi = h.epi[0] * 2 + h.epi[1]
                for s in range(h.steps):
                    g, kt = s // KT, s % KT
                    if g < h.maxima:
                        if kt == 0:
                            at_least(eng, max_split, (h.group0 + g + AHEAD - 1) * 2)
                        reduce_max(h, g, 2 * kt)
                        reduce_max(h, g, 2 * kt + 1)
                        if kt == KT - 1:
                            split_max(h, g)
                    if h.pro is not None:
                        if now := due(s, X_MOM, KT):
                            if now[0] == 0:
                                eng.wait_ge(x_loaded, (h.pro + 1) * 16)
                                eng.wait_ge(x_norm, RAISED + h.pro * (KT + 1))
                            moments(x_in, st_x, KT, x_mom, h.pro, *now)
                        if K_SPLIT <= s < K_SPLIT + SPLIT_OPS[0]:
                            split_k(h.pro, s - K_SPLIT)
                        if not h.scores and Q_SPLIT0 <= s < Q_SPLIT0 + SPLIT_OPS[1]:
                            split_q(h.pro, 0, s - Q_SPLIT0)
                    if h.pro1 is not None:
                        if h.scores and Q_SPLIT <= s < Q_SPLIT + SPLIT_OPS[1]:
                            split_q(h.pro1, 0, s - Q_SPLIT)
                        first = Q1_SPLIT if h.scores else Q1_ROT + 2
                        if first <= s < first + SPLIT_OPS[2]:
                            split_q(h.pro1, 1, s - first)
                    if h.epi is not None:
                        if s == 5:
                            divide(h, 3)
                        if now := due(s, A_MOM, ST):
                            if now[0] == 0:
                                eng.wait_ge(a_norm, RAISED + nth_epi * (ST + 2))
                            eng.wait_ge(ring_read, h.done("WO", now[0] // 2))
                            moments(act, st_a, ST, a_mom, nth_epi, *now)
                        if now := due(s, Y_MOM, ST):
                            if now[0] == 0:
                                eng.wait_ge(a_norm, RAISED + (nth_epi + 1) * (ST + 2))
                                eng.wait_ge(y_norm, RAISED + nth_epi * (ST + 1))
                            moments(res, st_y, ST, y_mom, nth_epi, *now)
                        if now := due(s, F_MOM, ST):
                            if now[0] == 0:
                                eng.wait_ge(biased, (nth_epi + 1) * ST)
                                eng.wait_ge(f_norm, RAISED + nth_epi * (ST + 2))
                            moments(act, st_f, ST, f_mom, nth_epi, *now)
                    if h.scores and s in (13, 21, 29):
                        divide(h, s // KT - 1)
            schedule(half, eng, prepare)


RAISED = 1
CONSTS = 9
WP_TURNED = 8


def rope_tables():
    import numpy as np
    inv = 1.0 / THETA ** (np.arange(0, D, 2, dtype=np.float32) / np.float32(D))
    ang = np.arange(S, dtype=np.float32)[None, :] * inv.astype(np.float32)[:, None]
    cs = np.stack([np.cos(ang), np.sin(ang)]).astype(np.float32)
    q = cs.reshape(2, H, NPAIR, S).transpose(0, 2, 1, 3).reshape(2, P, S)
    c, sn = (cs[i, :NPAIR].reshape(NPAIR, 2, HALF).transpose(1, 0, 2) for i in range(2))
    k = np.zeros((2, 2, NPAIR, HKV, 2, HALF), np.float32)
    k[:, :, :, :, 0] = c[:, None, :, None]
    k[:, 0, :, :, 1] = -sn[:, :, None]
    k[:, 1, :, :, 1] = sn[:, :, None]
    return np.ascontiguousarray(q), k.reshape(P, 2, HALF)


_INS = ["L0_attn_x", "L0_attn_Wq", "L0_attn_Wk", "L0_attn_Wv", "L0_attn_Wo", "L0_ffn_weight",
        "L0_ffn_alpha", "L0_ffn_bias"]


def kernel(**inputs):
    import numpy as np
    import concourse.bacc as bacc
    from concourse.bass_utils import run_bass_kernel_spmd as run

    nc = bacc.Bacc("TRN2", target_bir_lowering=False, num_devices=1)
    arrays = {f"in_{n}": np.ascontiguousarray(inputs[n]) for n in _INS}
    arrays["rope_q"], arrays["rope_k"] = rope_tables()
    args = [nc.dram_tensor(n, a.shape, F32, kind="ExternalInput").ap() for n, a in arrays.items()]
    out = nc.dram_tensor("out_0", (B, S, D), F32, kind="ExternalOutput").ap()
    sandwich_kernel(nc, *args, out)
    r = run(nc, [arrays], core_ids=[0])
    return r.results[0]["out_0"]
```

```python
import concourse.bass as bass
from concourse import mybir
from contextlib import ExitStack

F32 = mybir.dt.float32
BF16 = mybir.dt.bfloat16
ALU = mybir.AluOpType
ACT = mybir.ActivationFunctionType
AX = mybir.AxisListType

P = 128
B, S, D = 8, 1024, 256
H, HKV = 16, 4
G = H // HKV
HD = D // H
NPAIR = HD // 2
HALF = S // 2
KT = S // P
ST = HALF // P
DT = D // P
EPS = 1e-5
THETA = 10000.0
SCALE = float(D) ** -0.5
THRESH = 0.7

QPARTS = (0, 0, 1, 1, 0, 2)
KPARTS = (0, 1, 0, 1, 2, 0)
NBLK = len(QPARTS)
KROWS = NBLK * HD
MROWS = 2
RING = 3
PSLOTS = 4
LAG = 2
STEPS = HKV * KT
LEAD = 12
TURN = (-LEAD) % KT + 1
LAST = B - 1
NGROUP = 2 * HKV
FOLD = 2 * G * HALF // P
VCOLS = 2 * HD

PRO = {11: [("XT", 0, 0), ("XT", 1, 0)], 12: [("XT", 0, 1), ("XT", 1, 1)],
       13: [("K",)], 17: [("Q", 0, 0)], 18: [("Q", 0, 1)], 20: [("V",)]}
PRO1 = {5: [("Q", 1, 0)], 6: [("Q", 1, 1)]}
PRO1_LEAD = {4 - LEAD: [("Q", 1, 0)], 5 - LEAD: [("Q", 1, 1)]}
EPI = {8: [("WO", 0)], 9: [("WO", 1)],
       19: [("HT", 0), ("HT", 1)], 24: [("FF", 0)], 25: [("FF", 1)]}
X_MOM, A_MOM = (0, 1, 2, 5, 6, 7, 8, 8), (9, 9, 10, 10)
Y_MOM, F_MOM = (13, 14, 15, 16), (28, 28, 29, 30)
INVERT, SCALED = {22: 0, 4: -1}, {27: 0, 7: -1}
X_NORM, A_NORM, Y_NORM, ACT_SPLIT, BIAS, F_NORM = 9, 11, 17, 20, 26, 31
K_ROT, Q_ROT, Q1_ROT = 15, 27, 7
K_SPLIT, Q_SPLIT, Q1_SPLIT = (17, 18, 21, 22), (5, 6, 6, 8, 8, 9), (18, 21, 24, 24, 25, 25)
Q_ROT0, Q_SPLIT0 = 23, (24, 25, 26, 27, 28, 29)
K_SWAP = 14
K_STAGE = 22
Q_LOAD = 10
ROT_OPS = (3, 6, 6)
ROT_ALL = sum(ROT_OPS)
SPLIT_OPS = (4, 6, 6)
SPLIT_ALL = sum(SPLIT_OPS)
SPLIT_ACT = 3 * DT


class Half:

    def __init__(self, b, qc, scores=True, maxima=STEPS, turned=range(1, HKV + 1), pro=None, pro1=None,
                 epi=None, base=0, first=0, steps=STEPS, load_x=None, flush=True):
        self.b, self.qc = b, qc
        self.scores = scores
        self.maxima = maxima
        self.turned = turned
        self.pro = pro
        self.pro1 = pro1
        self.epi = epi
        self.base = base
        self.first = first
        self.steps = range(first, steps)
        self.load_x = load_x
        self.flush = flush
        self.alone = not scores and not maxima
        self.very_first = scores and not flush
        self.group0 = b * NGROUP + qc * HKV
        self.pair0 = b * (NGROUP // 2) + qc * (HKV // 2)
        self.place = {}
        n = 0
        for s in self.steps:
            if scores:
                for j in range(G):
                    self.place["ST", s, j] = n
                    n += 1
            for job in self.jobs(s):
                self.place[job] = n
                n += 1
        self.count = n

    def turns(self, s):
        return s % KT == TURN and s // KT + 1 in self.turned

    def jobs(self, s):
        out = [("MT", s // KT)] if self.turns(s) else []
        if self.pro is not None:
            out += PRO.get(s, [])
        if self.pro1 is not None:
            out += (PRO1 if self.scores else PRO1_LEAD).get(s, [])
        if self.epi is not None:
            out += EPI.get(s, [])
        return out

    def done(self, *job):
        return self.base + self.place[job] + 1


def sandwich_kernel(nc, x, wq, wk, wv, wo, wf, alpha, bias, rope_q, rope_k, out):
    ctx = ExitStack()
    with ctx:
        def sb(name, shape, dt):
            return ctx.enter_context(nc.sbuf_tensor(name, shape, dt))

        def sem(name):
            return ctx.enter_context(nc.semaphore(name))

        q_rows = sb("q_rows", [KROWS + MROWS, 2, H, HALF], BF16)
        k_rows = sb("k_rows", [KROWS + MROWS, HKV, S], BF16)
        k_next = sb("k_next", [KROWS, HKV, S], BF16)
        q_parts = sb("q_parts", [P, 3, 2, 2, HALF], BF16)
        k_parts = sb("k_parts", [P, 3, HALF], BF16)
        probs = sb("probs", [P, PSLOTS, G, HALF], F32)
        v_next = sb("v_next", [P, KT, HKV * HD], F32)
        v_cols = sb("v_cols", [P, HKV, KT, VCOLS], F32)
        row_max = sb("row_max", [P, 2, G * ST], F32)
        max_parts = sb("max_parts", [P, 2, MROWS, G * ST], BF16)
        max_rows = sb("max_rows", [MROWS * G * ST, 2, P], BF16)
        x_in = sb("x_in", [P, KT, D], F32)
        xT = sb("xT", [P, DT, S], F32)
        rot_in = sb("rot_in", [P, 2, 2, HALF], F32)
        rot_mul = sb("rot_mul", [P, 4, HALF], F32)
        rot_out = sb("rot_out", [P, 2, HALF], F32)
        cs_q = sb("cs_q", [P, 2, S], F32)
        cs_k = sb("cs_k", [P, 2, HALF], F32)
        heads = sb("heads", [P, 2, HALF], F32)
        pairs = sb("pairs", [P, DT, HALF], F32)
        sums = sb("sums", [P, DT, FOLD], F32)
        inv_sums = sb("inv_sums", [P, DT, FOLD], F32)
        inv_rows = sb("inv_rows", [P, DT, HALF], F32)
        inv_dram = nc.dram_tensor("inv_sums_dram", (DT, 2 * G, HALF), F32, kind="Internal").ap()
        attnT = sb("attnT", [P, DT, HALF], F32)
        actT = sb("actT", [P, DT, HALF], F32)
        act_parts = sb("act_parts", [P, 3, DT, HALF], BF16)
        act = sb("act", [P, ST, D], F32)
        res = sb("res", [P, ST, D], F32)
        wq_in = sb("wq_in", [P, DT, D], F32)
        wk_in = sb("wk_in", [P, DT, HKV * HD], F32)
        wv_sb = sb("wv_sb", [P, DT, HKV * HD], F32)
        wq_sb = sb("wq_sb", [P, DT, 2, NPAIR, H], F32)
        wk_sb = sb("wk_sb", [P, DT, 2, NPAIR, HKV], F32)
        wo_sb = sb("wo_sb", [P, DT, D], F32)
        wf_in = sb("wf_in", [P, DT, D], F32)
        wf_tern = sb("wf_tern", [P, DT, D], F32)
        wf_neg = sb("wf_neg", [P, DT, D], F32)
        wfT = sb("wfT", [P, DT, D], BF16)
        bias_sb = sb("bias_sb", [P, D], F32)
        alpha_sb = sb("alpha_sb", [P, 1], F32)
        abs_sum = sb("abs_sum", [P, 1], F32)
        delta = sb("delta", [P, 2], F32)
        ones = sb("ones", [P, P], F32)
        ident = sb("ident", [P, P], F32)
        ident_h = sb("ident_h", [P, P], BF16)
        m_half = sb("m_half", [P, KT], F32)

        def stats(name, n):
            return (sb(f"{name}_bn", [P, n, 6], F32), sb(f"{name}_mv", [P, n, 2], F32),
                    sb(f"{name}_nm", [P, n], F32), sb(f"{name}_ve", [P, n], F32),
                    sb(f"{name}_rs", [P, n], F32))

        st_x, st_a, st_y, st_f = stats("sx", KT), stats("sa", ST), stats("sy", ST), stats("sf", ST)

        ring = ctx.enter_context(nc.psum_tensor("ring", [P, RING, 512], F32))
        smax = ctx.enter_context(nc.psum_tensor("smax", [P, 2, 2, 512], F32))
        pv = ctx.enter_context(nc.psum_tensor("pv", [P, 512], F32))

        passed = sem("passed")
        proj_loaded = sem("proj_loaded")
        late_loaded = sem("late_loaded")
        consts = sem("consts")
        w_cols = sem("w_cols")
        w_prep = sem("w_prep")
        abs_done = sem("abs_done")
        x_loaded = sem("x_loaded")
        res_loaded = sem("res_loaded")
        ring_full = sem("ring_full")
        ring_read = sem("ring_read")
        max_full = sem("max_full")
        max_read = sem("max_read")
        max_split = sem("max_split")
        max_loaded = sem("max_loaded")
        pv_step = sem("pv_step")
        heads_read = sem("heads_read")
        heads_moved = sem("heads_moved")
        inverted = sem("inverted")
        inv_stored = sem("inv_stored")
        inv_spread = sem("inv_spread")
        v_ready = sem("v_ready")
        x_mom = sem("x_mom")
        a_mom = sem("a_mom")
        y_mom = sem("y_mom")
        f_mom = sem("f_mom")
        x_norm = sem("x_norm")
        a_norm = sem("a_norm")
        y_norm = sem("y_norm")
        f_norm = sem("f_norm")
        act_part = sem("act_part")
        act_split = sem("act_split")
        biased = sem("biased")
        rot_step = sem("rot_step")
        parts_step = sem("parts_step")
        q_loaded = [sem("q_loaded0"), sem("q_loaded1")]
        k_swapped = sem("k_swapped")
        k_staged = sem("k_staged")
        k_loaded = [sem(f"k_loaded{g}") for g in range(HKV)]
        divided = sem("divided")
        stored = sem("stored")

        def schedule(half, eng, prepare=None):
            h = Half(0, 0, scores=False, maxima=0, turned=(), pro=0, flush=False)
            half(h)
            at = h.count
            if prepare:
                prepare(at)
            h = Half(0, 0, scores=False, turned=(0,), base=at, first=-LEAD, steps=0,
                     load_x=1, pro1=0, flush=False)
            half(h)
            at += h.count
            h = Half(0, 0, pro=1, base=at, flush=False)
            half(h)
            at += h.count
            n1 = Half(0, 1, pro1=0, epi=(0, 0)).count
            n0 = Half(0, 0, pro=0, epi=(0, 0)).count
            with eng.Fori(0, B - 2) as b:
                base = b * (n1 + n0) + at
                half(Half(b, 1, pro1=b + 1, epi=(b, 0), base=base, load_x=b + 2))
                half(Half(b + 1, 0, pro=b + 2, epi=(b, 1), base=base + n1))
            at += (B - 2) * (n1 + n0)
            h = Half(B - 2, 1, pro1=LAST, epi=(B - 2, 0), base=at)
            half(h)
            at += h.count
            h = Half(LAST, 0, epi=(B - 2, 1), base=at)
            half(h)
            at += h.count
            h = Half(LAST, 1, epi=(LAST, 0), maxima=STEPS - LEAD, turned=range(1, HKV), base=at)
            half(h)
            at += h.count
            h = Half(B, 0, scores=False, maxima=0, turned=(), epi=(B - 1, 1), base=at)
            half(h)

        def at_least(eng, s, value):
            if not isinstance(value, int) or value > 0:
                eng.wait_ge(s, value)

        def root(eng, st, n, mom, norm, nth):
            _, _, _, ve, rs = st
            eng.wait_ge(mom, (nth + 1) * (2 * n + 2))
            eng.tensor_tensor(rs[:, :], ve[:, :], m_half[:, 0:n], ALU.pow).then_inc(norm, 1)

        def normalise(eng, dst, src, st, n, norm, nth, per):
            _, _, nm, _, rs = st
            eng.wait_ge(norm, RAISED + nth * per + 1)
            eng.sem_inc(passed, 1)
            for t in range(n):
                eng.tensor_scalar(dst[:, t, :], src[:, t, :], nm[:, t:t + 1], rs[:, t:t + 1],
                                  ALU.add, ALU.mult).then_inc(norm, 1)

        def rotate_k(eng, h):
            own, other = rot_in[:, 0, 0, :], rot_in[:, 0, 1, :]
            eng.wait_ge(k_swapped, (h.pro + 1) * 4 * 16)
            at_least(eng, rot_step, h.pro * ROT_ALL)
            eng.tensor_tensor(rot_mul[:, 0, :], own, cs_k[:, 0, :], ALU.mult).then_inc(rot_step, 1)
            eng.tensor_tensor(rot_mul[:, 1, :], other, cs_k[:, 1, :], ALU.mult).then_inc(rot_step, 1)
            eng.wait_ge(rot_step, h.pro * ROT_ALL + 2)
            at_least(eng, parts_step, h.pro * SPLIT_ALL)
            eng.tensor_tensor(rot_out[:, 0, :], rot_mul[:, 0, :], rot_mul[:, 1, :],
                              ALU.add).then_inc(rot_step, 1)

        def rotate_q(eng, h, row, a):
            cs = cs_q[:, :, a * HALF:(a + 1) * HALF]
            even, odd = rot_in[:, 1, 0, :], rot_in[:, 1, 1, :]
            before = row * ROT_ALL + sum(ROT_OPS[:a + 1])
            eng.wait_ge(ring_read, h.done("Q", a, 1))
            eng.wait_ge(rot_step, before)
            eng.tensor_tensor(rot_mul[:, 0, :], even, cs[:, 0, :], ALU.mult).then_inc(rot_step, 1)
            eng.tensor_tensor(rot_mul[:, 1, :], odd, cs[:, 1, :], ALU.mult).then_inc(rot_step, 1)
            eng.tensor_tensor(rot_mul[:, 2, :], even, cs[:, 1, :], ALU.mult).then_inc(rot_step, 1)
            eng.tensor_tensor(rot_mul[:, 3, :], odd, cs[:, 0, :], ALU.mult).then_inc(rot_step, 1)
            eng.wait_ge(rot_step, before + 4)
            eng.wait_ge(parts_step, row * SPLIT_ALL + sum(SPLIT_OPS[:a + 1]))
            eng.tensor_tensor(rot_out[:, 0, :], rot_mul[:, 0, :], rot_mul[:, 1, :],
                              ALU.subtract).then_inc(rot_step, 1)
            eng.tensor_tensor(rot_out[:, 1, :], rot_mul[:, 2, :], rot_mul[:, 3, :],
                              ALU.add).then_inc(rot_step, 1)

        def norm_attention(eng, nth):
            normalise(eng, act, act, st_a, ST, a_norm, nth, ST + 2)
            eng.wait_ge(a_norm, RAISED + nth * (ST + 2) + ST + 1)
            eng.wait_ge(res_loaded, (nth + 1) * 16)
            eng.tensor_tensor(res[:, :, :], res[:, :, :], act[:, :, :], ALU.add).then_inc(a_norm, 1)

        def split_act(eng, h, nth):
            at = nth * SPLIT_ACT
            for dt in range(DT):
                src, dst = actT[:, dt, :], [act_parts[:, m, dt, :] for m in range(3)]
                eng.wait_ge(act_part, nth + 1)
                eng.tensor_tensor(src, src, dst[0], ALU.subtract).then_inc(act_split, 1)
                eng.wait_ge(act_split, at + dt * 3 + 1)
                eng.sem_inc(passed, 1)
                eng.tensor_copy(dst[1], src).then_inc(act_split, 1)
                eng.wait_ge(act_split, at + dt * 3 + 2)
                eng.tensor_tensor(dst[2], src, dst[1], ALU.subtract).then_inc(act_split, 1)

        def add_bias(eng, h):
            for t in range(ST):
                if t % 2 == 0:
                    eng.wait_ge(ring_read, h.done("FF", t // 2))
                eng.tensor_tensor(act[:, t, :], act[:, t, :], bias_sb[:, :], ALU.add).then_inc(biased, 1)

        def norm_forward(eng, nth):
            normalise(eng, act, act, st_f, ST, f_norm, nth, ST + 2)
            eng.wait_ge(f_norm, RAISED + nth * (ST + 2) + ST + 1)
            eng.tensor_tensor(res[:, :, :], res[:, :, :], act[:, :, :], ALU.add).then_inc(f_norm, 1)

        def scale_heads(eng, h, pair):
            eng.wait_ge(inv_spread, (h.pair0 + pair + 1) * 16)
            if pair < 0:
                eng.wait_ge(ring_full, h.base)
            elif h.epi is not None:
                eng.wait_ge(ring_full, h.done("WO", 1))
            eng.sem_inc(passed, 1)
            eng.tensor_tensor(attnT[:, pair % DT, :], pairs[:, pair % DT, :], inv_rows[:, pair % DT, :], ALU.mult)\
               .then_inc(divided, 1)

        def roots(eng, h, s):
            if h.pro is not None and s == X_NORM:
                root(eng, st_x, KT, x_mom, x_norm, h.pro)
            if h.epi is not None:
                nth = h.epi[0] * 2 + h.epi[1]
                for at, st, mom, norm in ((A_NORM, st_a, a_mom, a_norm), (Y_NORM, st_y, y_mom, y_norm),
                                          (F_NORM, st_f, f_mom, f_norm)):
                    if s == at:
                        root(eng, st, ST, mom, norm, nth)

        def between(eng, h, s):
            if s in SCALED and (h.scores if SCALED[s] >= 0 else h.flush):
                scale_heads(eng, h, SCALED[s])
            if h.pro is not None:
                if s == X_NORM:
                    normalise(eng, x_in, x_in, st_x, KT, x_norm, h.pro, KT + 1)
                if s == K_ROT:
                    rotate_k(eng, h)
                if s == (Q_ROT0 if h.alone else Q_ROT):
                    rotate_q(eng, h, h.pro, 0)
            if h.pro1 is not None and s == (Q1_ROT if h.scores else 6 - LEAD):
                rotate_q(eng, h, h.pro1, 1)
            if h.epi is not None:
                nth = h.epi[0] * 2 + h.epi[1]
                if s == A_NORM:
                    norm_attention(eng, nth)
                if s == Y_NORM:
                    normalise(eng, act, res, st_y, ST, y_norm, nth, ST + 1)
                if s == ACT_SPLIT:
                    split_act(eng, h, nth)
                if s == BIAS:
                    add_bias(eng, h)
                if s == F_NORM:
                    norm_forward(eng, nth)

        block = ctx.enter_context(nc.Block())

        @block.sync
        def _(eng):
            eng.sem_inc(stored, RAISED)
            eng.dma_start(x_in[:, :, :], x[0, :, :].rearrange("(t p) d -> p t d", p=P)).then_inc(x_loaded, 16)
            for dst, src in ((wk_in, wk), (wq_in, wq), (wv_sb, wv)):
                eng.dma_start(dst[:, :, :], src.rearrange("(t p) n -> p t n", p=P)).then_inc(proj_loaded, 16)
            eng.dma_start(cs_k[:, :, :], rope_k).then_inc(proj_loaded, 16)
            eng.dma_start(cs_q[:, :, :], rope_q.rearrange("c p s -> p c s")).then_inc(proj_loaded, 16)
            for dst, src in ((wf_in, wf), (wo_sb, wo)):
                eng.dma_start(dst[:, :, :], src.rearrange("(t p) n -> p t n", p=P)).then_inc(late_loaded, 16)
            eng.dma_start(bias_sb[:, :], bias.partition_broadcast(P)).then_inc(late_loaded, 16)
            eng.dma_start(alpha_sb[:, :], alpha.partition_broadcast(P)).then_inc(late_loaded, 16)

            def load_q(b, qc):
                before = b * SPLIT_ALL + sum(SPLIT_OPS[:1 + qc])
                for part, ready in ((0, 1), (1, 4), (2, 6)):
                    eng.wait_ge(parts_step, before + ready)
                    for blk, eo in [(m, eo) for m in range(NBLK) if QPARTS[m] == part for eo in range(2)]:
                        r = blk * HD + eo * NPAIR
                        eng.dma_start(q_rows[r:r + NPAIR, qc, :, :],
                                      q_parts[:, part, eo, qc, :]).then_inc(q_loaded[qc], 16)

            def stage_k(b):
                for g in range(HKV):
                    at_least(eng, k_loaded[g], b * 16)
                eng.sem_inc(passed, 1)
                place_k(b, k_next)

            def swap_k(h):
                eng.wait_ge(ring_read, h.done("K"))
                eng.sem_inc(passed, 1)
                for tile in range(4):
                    own, other = tile * NPAIR * HKV, (tile ^ 1) * NPAIR * HKV
                    eng.dma_start(rot_in[own:own + NPAIR * HKV, 0, 1, :],
                                  rot_in[other:other + NPAIR * HKV, 0, 0, :]).then_inc(k_swapped, 16)

            def place_k(b, dst):
                for part, ready in ((0, 1), (1, 3), (2, 4)):
                    eng.wait_ge(parts_step, b * SPLIT_ALL + ready)
                    for blk, a in [(m, a) for m in range(NBLK) if KPARTS[m] == part for a in range(2)]:
                        eng.dma_start(dst[blk * HD:(blk + 1) * HD, :, a * HALF:(a + 1) * HALF],
                                      k_parts[a * P // 2:(a + 1) * P // 2, part, :]).then_inc(k_staged, 16)

            def take_k(b, g):
                eng.wait_ge(k_staged, (b + 1) * 16 * 2 * NBLK)
                eng.dma_start(k_rows[0:KROWS, g, :], k_next[:, g, :]).then_inc(k_loaded[g], 16)

            def load_res(b, qc):
                eng.wait_ge(stored, RAISED + (b * 2 + qc) * 16)
                eng.dma_start(res[:, :, :], x[bass.ds(b, 1), qc * HALF:(qc + 1) * HALF, :]
                              .rearrange("a (t p) d -> p (a t) d", p=P)).then_inc(res_loaded, 16)

            def move_heads(h, g):
                eng.wait_ge(heads_read, h.group0 + g + 1)
                eng.sem_inc(passed, 1)
                at_least(eng, heads_moved, (h.group0 + g) * 32)
                eng.sem_inc(passed, 1)
                if g % 2 == 0:
                    at_least(eng, divided, h.pair0 + g // 2 - 1)
                    eng.sem_inc(passed, 1)
                r = g % 2 * (P // 2)
                eng.dma_start(pairs[r:r + P // 2, g // 2 % 2, :], heads[0:P:2, g % 2, :])\
                   .then_inc(heads_moved, 16)
                eng.dma_start(sums[r:r + P // 2, g // 2 % 2, :], heads[1:P:VCOLS, g % 2, :])\
                   .then_inc(heads_moved, 16)

            def spread_inverses(h, pair):
                eng.wait_ge(inverted, h.pair0 + pair + 1)
                eng.sem_inc(passed, 1)
                at_least(eng, divided, h.pair0 + pair)
                eng.sem_inc(passed, 1)
                eng.dma_start(inv_dram[pair % DT, :, :].rearrange("j (k n) -> (j k) n", n=FOLD),
                              inv_sums[:, pair % DT, :]).then_inc(inv_stored, 16)
                eng.wait_ge(inv_stored, (h.pair0 + pair + 1) * 16)
                eng.sem_inc(passed, 1)
                eng.dma_start(inv_rows[:, pair % DT, :],
                              inv_dram[pair % DT, :, :].unsqueeze(1).broadcast_to([2 * G, HD, HALF]))\
                   .then_inc(inv_spread, 16)

            def half(h):
                if h.load_x is not None:
                    eng.wait_ge(ring_full, h.base)
                    eng.sem_inc(passed, 1)
                    eng.dma_start(x_in[:, :, :], x[bass.ds(h.load_x, 1), :, :]
                                  .rearrange("a (t p) d -> p (a t) d", p=P)).then_inc(x_loaded, 16)
                if h.epi is not None:
                    load_res(*h.epi)
                if h.scores or h.flush:
                    eng.wait_ge(ring_full, h.base)
                    eng.sem_inc(passed, 1)
                if h.scores and h.qc == 0 and h.flush:
                    take_k(h.b, HKV - 1)
                for s in h.steps:
                    if s % KT == LAG and ((s > LAG and h.scores) or (s == LAG and h.flush)):
                        move_heads(h, s // KT - 1)
                    if s in INVERT and (h.scores if INVERT[s] >= 0 else h.flush):
                        spread_inverses(h, INVERT[s])
                    if s == Q_LOAD and h.scores and h.pro1 is not None:
                        load_q(h.pro1, 0)
                    if s == Q_LOAD and h.scores and h.qc == 0:
                        load_q(h.b, 1)
                    if h.turns(s):
                        nxt = h.qc * HKV + s // KT + 1
                        qc, g = nxt // HKV % 2, nxt % HKV
                        eng.wait_ge(ring_read, h.done("MT", s // KT))
                        eng.dma_start(q_rows[KROWS:KROWS + MROWS, qc, g * G:(g + 1) * G, :],
                                      max_rows[:, nxt % 2, :]).then_inc(max_loaded, 16)
                    if h.scores and h.qc == 1 and s % KT == 0 and s > 0 and h.b is not LAST:
                        eng.wait_ge(ring_full, h.done("ST", s - 1, G - 1))
                        take_k(h.b + 1, s // KT - 1)
                    if h.pro is not None and s == K_SWAP:
                        swap_k(h)
                    if h.pro is not None and s == K_STAGE:
                        if h.alone:
                            place_k(0, k_rows)
                        else:
                            stage_k(h.pro)
                    if h.epi is not None and s == STEPS - 1:
                        eb, eq = h.epi
                        eng.wait_ge(f_norm, RAISED + (eb * 2 + eq + 1) * (ST + 2))
                        eng.dma_start(out[bass.ds(eb, 1), eq * HALF:(eq + 1) * HALF, :]
                                      .rearrange("a (t p) d -> p (a t) d", p=P), res[:, :, :])\
                           .then_inc(stored, 16)
                if h.alone and h.pro is not None:
                    load_q(0, 0)
                    eng.wait_ge(k_staged, 16 * 2 * NBLK)
                    for g in range(HKV):
                        eng.sem_inc(k_loaded[g], 16)

            schedule(half, eng)
            eng.wait_ge(stored, RAISED + 2 * B * 16)

        @block.gpsimd
        def _(eng):
            for s in (x_norm, a_norm, y_norm, f_norm):
                eng.sem_inc(s, RAISED)
            eng.memset(ident[:, :], 0.0).then_inc(consts, 1)
            eng.memset(ident_h[:, :], 0.0).then_inc(consts, 1)
            eng.wait_ge(consts, 2)
            for m in (ident, ident_h):
                eng.affine_select(out=m[:, :], in_=m[:, :], compare_op=ALU.not_equal, fill=1.0, base=0,
                                  pattern=[[-1, P]], channel_multiplier=1).then_inc(consts, 1)
            eng.memset(ones[:, :], 1.0).then_inc(consts, 1)
            eng.memset(m_half[:, :], -0.5).then_inc(consts, 1)
            eng.wait_ge(consts, 6)
            eng.memset(k_rows[KROWS:KROWS + MROWS, :, :], -1.0).then_inc(consts, 1)
            eng.wait_ge(consts, 7)
            eng.memset(v_cols[:, :, :, :], 1.0).then_inc(consts, 1)
            eng.wait_ge(consts, CONSTS)

            def take_v(h, b, g):
                eng.sem_inc(passed, 1)
                eng.tensor_copy(v_cols[:, g, :, :].rearrange("p k (c v) -> p k c v", v=2)[:, :, :, 0], v_next[:, :, g * HD:(g + 1) * HD])\
                   .then_inc(v_ready, 1)

            def half(h):
                for s in h.steps:
                    if h.scores and h.flush and h.qc == 0 and s == 3:
                        eng.wait_ge(pv_step, h.group0 * KT)
                        take_v(h, h.b, HKV - 1)
                    if h.scores and h.qc == 1 and s % KT == 3 and s > KT and h.b is not LAST:
                        g = s // KT - 1
                        eng.wait_ge(pv_step, (h.group0 + g + 1) * KT)
                        take_v(h, h.b + 1, g)
                    if h.alone and h.pro is not None and s == K_ROT:
                        eng.wait_ge(ring_read, h.done("V"))
                        for g in range(HKV):
                            take_v(h, 0, g)
                    roots(eng, h, s)
                    if not h.alone:
                        between(eng, h, s)

            def prepare(at):
                eng.wait_ge(proj_loaded, 5 * 16)
                eng.wait_ge(late_loaded, 4 * 16)

            schedule(half, eng, prepare)

        @block.scalar
        def _(eng):
            def prepare(at):
                eng.wait_ge(late_loaded, 4 * 16)
                eng.activation(wf_neg[:, :, :], wf_in[:, :, :], ACT.Abs, accum_out=abs_sum[:, :])\
                   .then_inc(abs_done, 1)
                eng.wait_ge(w_prep, WP_TURNED)
                eng.activation(wfT[:, 0, :], ring[:, 0, 0:D], ACT.Copy).then_inc(abs_done, 1)
                eng.activation(wfT[:, 1, :], ring[:, 0, D:2 * D], ACT.Copy).then_inc(abs_done, 1)

            def move(dst, src):
                eng.activation(dst, src, ACT.Copy).then_inc(ring_read, 1)

            def half(h):
                n = 0
                for s in h.steps:
                    if s % KT == LAG and ((s > LAG and h.scores) or (s == LAG and h.flush)):
                        read_heads(h, s // KT - 1)
                    if h.scores:
                        step = h.group0 * KT + s
                        at_least(eng, pv_step, step - PSLOTS + 1)
                        for j in range(G):
                            eng.wait_ge(ring_full, h.done("ST", s, j))
                            eng.activation(probs[:, s % PSLOTS, j, :], ring[:, n % RING, :], ACT.Exp,
                                           scale=SCALE).then_inc(ring_read, 1)
                            n += 1
                    for job in h.jobs(s):
                        kind, a = job[0], job[1:]
                        src = ring[:, n % RING, :]
                        eng.wait_ge(ring_full, h.done(*job))
                        if kind == "MT":
                            par = (a[0] + 1) % 2
                            at_least(eng, max_loaded, (h.group0 + a[0]) * 16)
                            move(max_rows[:, par, :], src[0:MROWS * G * ST, 0:P // 2].bitcast(BF16))
                        elif kind == "XT":
                            move(xT[:, a[0], a[1] * HALF:(a[1] + 1) * HALF], src)
                        elif kind == "K":
                            at_least(eng, rot_step, (h.pro - 1) * ROT_ALL + 2)
                            move(rot_in[:, 0, 0, :], src)
                        elif kind == "Q":
                            row = h.pro1 if a[0] else h.pro
                            at_least(eng, rot_step, row * ROT_ALL + (7 if a[0] else -2))
                            move(rot_in[:, 1, a[1], :], src)
                        elif kind == "V":
                            at_least(eng, v_ready, h.pro * HKV)
                            move(v_next[:, :, :].rearrange("p t n -> p (t n)"), src)
                        elif kind == "HT":
                            move(actT[:, a[0], :], src)
                        elif kind == "WO":
                            eng.wait_ge(f_norm, RAISED + (h.epi[0] * 2 + h.epi[1]) * (ST + 2))
                            move(act[:, 2 * a[0]:2 * a[0] + 2, :].rearrange("p t n -> p (t n)"), src)
                        elif kind == "FF":
                            eng.activation(act[:, 2 * a[0]:2 * a[0] + 2, :].rearrange("p t n -> p (t n)"),
                                           src, ACT.Copy, scale=alpha_sb[:, 0:1]).then_inc(ring_read, 1)
                        n += 1

            def read_heads(h, g):
                nth = h.group0 + g
                eng.wait_ge(pv_step, (nth + 1) * KT)
                at_least(eng, heads_moved, (nth - 1) * 32)
                eng.activation(heads[:, g % 2, :], pv[:, :], ACT.Copy).then_inc(heads_read, 1)

            schedule(half, eng, prepare)

        @block.tensor
        def _(eng):
            eng.wait_ge(consts, CONSTS)
            for _ in range(WARM):
                eng.matmul(smax[:, 0, 0, 0:P], ident[:, :], ident[:, :], start=True, stop=True)
            def prepare(at):
                eng.wait_ge(ring_read, at)
                eng.wait_ge(abs_done, 1)
                eng.matmul(ring[:, 1, 0:1], ones[:, :], abs_sum[:, :], start=True, stop=True)\
                   .then_inc(w_prep, 1)
                eng.wait_ge(w_prep, WP_TURNED - 1)
                for dt in range(DT):
                    for ot in range(DT):
                        mm = eng.transpose(ring[:, 0, dt * D + ot * P:dt * D + (ot + 1) * P],
                                           wf_tern[:, ot, dt * P:(dt + 1) * P], ident[:, :])
                mm.then_inc(w_prep, 1)
                eng.wait_ge(abs_done, 3)

            def maxima(h, g, unit):
                nth = h.group0 + g
                at = h.qc * HKV + g
                qc, kv, row = at // HKV % 2, at % HKV, h.b + at // NGROUP
                if unit == 0:
                    eng.wait_ge(q_loaded[qc], (row + 1) * 16 * 2 * NBLK)
                    eng.wait_ge(k_loaded[kv], (row + 1) * 16)
                at_least(eng, max_read, nth * G * ST + unit - 1)
                j, qt = unit // ST, unit % ST
                for c in range(2):
                    mm = eng.matmul(smax[:, unit % 2, c, :],
                                    q_rows[0:KROWS, qc, kv * G + j, qt * P:(qt + 1) * P],
                                    k_rows[0:KROWS, kv, c * 512:(c + 1) * 512], start=True, stop=True)
                mm.then_inc(max_full, 1)

            def values(h, s):
                step = h.group0 * KT + s
                g, kt = s // KT % HKV, s % KT
                if kt == 0:
                    at_least(eng, heads_read, h.group0 + s // KT)
                    if h.qc == 0:
                        eng.wait_ge(v_ready, h.b * HKV + g + 1)
                if s >= 0:
                    eng.wait_ge(ring_read, h.done("ST", s, G - 1))
                else:
                    eng.wait_ge(ring_read, h.base)
                for j in range(G):
                    mm = eng.matmul(pv[j * VCOLS:(j + 1) * VCOLS, :], v_cols[:, g, kt, :],
                                    probs[:, s % PSLOTS, j, :], start=(kt == 0), stop=(kt == KT - 1),
                                    skip_group_check=True)
                mm.then_inc(pv_step, 1)

            def half(h):
                n = 0
                for s in h.steps:
                    g, kt = s // KT, s % KT
                    mg, mkt = (s + LEAD) // KT, (s + LEAD) % KT
                    for j in range(G):
                        if j == 0 and h.scores and kt == 0:
                            eng.wait_ge(max_loaded, (h.group0 + g + 1) * 16)
                        if h.scores:
                            at_least(eng, ring_read, h.base + (n - RING + 1 if n >= RING else 0))
                            eng.matmul(ring[:, n % RING, :],
                                       k_rows[:, g, kt * P:(kt + 1) * P],
                                       q_rows[:, h.qc, g * G + j, :], start=True, stop=True)\
                               .then_inc(ring_full, 1)
                            n += 1
                        if j in (0, 2) and s < h.maxima:
                            maxima(h, mg, mkt * 2 + j // 2)
                    if (h.scores and s >= LAG) or (h.flush and s < LAG):
                        values(h, s - LAG)
                    for job in h.jobs(s):
                        kind, a = job[0], job[1:]
                        dst = ring[:, n % RING, :]
                        at_least(eng, ring_read, h.base + (n - RING + 1 if n >= RING else 0))
                        if kind == "MT":
                            nth = h.group0 + a[0] + 1
                            par = (a[0] + 1) % 2
                            eng.wait_ge(max_split, (nth + 1) * 2)
                            mm = eng.transpose(dst[0:MROWS * G * ST, 0:P // 2].bitcast(BF16),
                                               max_parts[:, par, :, :].rearrange("p m n -> p (m n)"),
                                               ident_h[:, :])
                        elif kind == "XT":
                            eng.wait_ge(x_norm, RAISED + (h.pro + 1) * (KT + 1))
                            for t in range(ST):
                                mm = eng.transpose(dst[:, t * P:(t + 1) * P],
                                                   x_in[:, a[1] * ST + t, a[0] * P:(a[0] + 1) * P],
                                                   ident[:, :])
                        elif kind == "K":
                            if h.alone:
                                eng.wait_ge(proj_loaded, 5 * 16)
                                eng.wait_ge(w_cols, 4 * DT)
                            eng.wait_ge(ring_read, h.done("XT", 1, 1))
                            for dt in range(DT):
                                for half_of, eo in ((0, 0), (0, 1), (1, 0), (1, 1)):
                                    tile = (half_of * 2 + eo) * NPAIR * HKV
                                    mm = eng.matmul(dst[tile:tile + NPAIR * HKV, :],
                                                    wk_sb[:, dt, eo, :, :].rearrange("p i h -> p (i h)"),
                                                    xT[:, dt, half_of * HALF:(half_of + 1) * HALF],
                                                    start=(dt == 0), stop=(dt == DT - 1),
                                                    skip_group_check=True)
                        elif kind == "Q":
                            for dt in range(DT):
                                mm = eng.matmul(dst, wq_sb[:, dt, a[1], :, :].rearrange("p i h -> p (i h)"),
                                                xT[:, dt, a[0] * HALF:(a[0] + 1) * HALF],
                                                start=(dt == 0), stop=(dt == DT - 1))
                        elif kind == "V":
                            for t in range(KT):
                                for dt in range(DT):
                                    mm = eng.matmul(dst[:, t * HKV * HD:(t + 1) * HKV * HD],
                                                    xT[:, dt, t * P:(t + 1) * P], wv_sb[:, dt, :],
                                                    start=(dt == 0), stop=(dt == DT - 1))
                        elif kind == "HT":
                            eng.wait_ge(y_norm, RAISED + (h.epi[0] * 2 + h.epi[1] + 1) * (ST + 1))
                            for t in range(ST):
                                mm = eng.transpose(dst[:, t * P:(t + 1) * P],
                                                   act[:, t, a[0] * P:(a[0] + 1) * P], ident[:, :])
                        elif kind == "WO":
                            eng.wait_ge(divided, (h.epi[0] * 2 + h.epi[1] + 1) * 2)
                            for t in range(2):
                                for dt in range(DT):
                                    mm = eng.matmul(dst[:, t * D:(t + 1) * D],
                                                    attnT[:, dt, (2 * a[0] + t) * P:(2 * a[0] + t + 1) * P],
                                                    wo_sb[:, dt, :], start=(dt == 0), stop=(dt == DT - 1))
                        elif kind == "FF":
                            eng.wait_ge(act_split, (h.epi[0] * 2 + h.epi[1] + 1) * SPLIT_ACT)
                            for t in range(2):
                                for k in range(3 * DT):
                                    m, dt = k // DT, k % DT
                                    mm = eng.matmul(dst[:, t * D:(t + 1) * D],
                                                    act_parts[:, m, dt, (2 * a[0] + t) * P:(2 * a[0] + t + 1) * P],
                                                    wfT[:, dt, :], start=(k == 0), stop=(k == 3 * DT - 1))
                        mm.then_inc(ring_full, 1)
                        n += 1

            schedule(half, eng, prepare)

        @block.vector
        def _(eng):
            def part_columns():
                eng.wait_ge(proj_loaded, 5 * 16)
                for dt in range(DT):
                    for eo in range(2):
                        eng.tensor_copy(wq_sb[:, dt, eo, :, :],
                                        wq_in[:, dt, :].rearrange("p (h i e) -> p e i h", h=H, e=2)[:, eo])\
                           .then_inc(w_cols, 1)
                        eng.tensor_copy(wk_sb[:, dt, eo, :, :],
                                        wk_in[:, dt, :].rearrange("p (h i e) -> p e i h", h=HKV, e=2)[:, eo])\
                           .then_inc(w_cols, 1)
            eng.wait_ge(consts, CONSTS)

            def prepare(at):
                eng.wait_ge(late_loaded, 4 * 16)
                eng.wait_ge(w_prep, 1)
                eng.tensor_scalar(delta[:, 0:1], ring[:, 1, 0:1], 1.0 / (D * D), THRESH, ALU.mult, ALU.mult)\
                   .then_inc(w_prep, 1)
                eng.wait_ge(w_prep, 2)
                eng.tensor_scalar(delta[:, 1:2], delta[:, 0:1], -1.0, None, ALU.mult).then_inc(w_prep, 1)
                eng.wait_ge(w_prep, 3)
                eng.tensor_scalar(wf_tern[:, :, :], wf_in[:, :, :], delta[:, 0:1], None, ALU.is_gt)\
                   .then_inc(w_prep, 1)
                eng.tensor_scalar(wf_neg[:, :, :], wf_in[:, :, :], delta[:, 1:2], None, ALU.is_lt)\
                   .then_inc(w_prep, 1)
                eng.wait_ge(w_prep, 5)
                eng.tensor_tensor(wf_tern[:, :, :], wf_tern[:, :, :], wf_neg[:, :, :], ALU.subtract)\
                   .then_inc(w_prep, 1)

            def moments(src, st, n, mom, nth, t, tiles):
                bn, mv, nm, ve, _ = st
                at = nth * (2 * n + 2)
                for i in range(t, t + tiles):
                    eng.bn_stats(bn[:, i, :], src[:, i, :]).then_inc(mom, 1)
                if t + tiles == n:
                    eng.wait_ge(mom, at + n)
                    eng.sem_inc(passed, 1)
                    for i in range(n):
                        eng.bn_aggr(mv[:, i, :], bn[:, i, :]).then_inc(mom, 1)
                    eng.wait_ge(mom, at + 2 * n)
                    eng.tensor_scalar(nm[:, :], mv[:, :, 0], -1.0, None, ALU.mult).then_inc(mom, 1)
                    eng.tensor_scalar(ve[:, :], mv[:, :, 1], EPS, None, ALU.add).then_inc(mom, 1)

            def split_k(row, i):
                src, dst = rot_out[:, 0, :], [k_parts[:, m, :] for m in range(3)]
                before = row * SPLIT_ALL
                if i == 0:
                    eng.wait_ge(rot_step, row * ROT_ALL + ROT_OPS[0])
                    at_least(eng, k_staged, row * 16 * 2 * NBLK)
                    eng.tensor_copy(dst[0], src).then_inc(parts_step, 1)
                else:
                    eng.wait_ge(parts_step, before + i)
                    if i == 2:
                        eng.tensor_copy(dst[1], src).then_inc(parts_step, 1)
                    else:
                        out_ = src if i == 1 else dst[2]
                        eng.tensor_tensor(out_, src, dst[i // 2], ALU.subtract).then_inc(parts_step, 1)

            def split_q(row, a, i):
                src, dst = rot_out[:, :, :], [q_parts[:, m, :, a, :] for m in range(3)]
                before = row * SPLIT_ALL + sum(SPLIT_OPS[:a + 1])
                if i == 0:
                    eng.wait_ge(rot_step, row * ROT_ALL + sum(ROT_OPS[:a + 2]))
                    at_least(eng, q_loaded[a], row * 16 * 2 * NBLK)
                    eng.tensor_copy(dst[0], src).then_inc(parts_step, 1)
                elif i == 3:
                    eng.wait_ge(parts_step, before + 3)
                    eng.tensor_copy(dst[1], src).then_inc(parts_step, 1)
                else:
                    eo = (i - 1) % 3
                    eng.wait_ge(parts_step, before + i - eo)
                    out_ = src if i < 3 else dst[2]
                    eng.tensor_tensor(out_[:, eo, :], src[:, eo, :], dst[i // 3][:, eo, :], ALU.subtract)\
                       .then_inc(parts_step, 1)

            def pieces(s, when):
                return [i for i, at in enumerate(when) if at == s]

            def due(s, when):
                return (when.index(s), when.count(s)) if s in when else None

            def reduce_max(h, g, unit):
                eng.wait_ge(max_full, (h.group0 + g) * G * ST + unit + 1)
                eng.tensor_reduce(row_max[:, g % 2, unit:unit + 1],
                                  smax[:, unit % 2, :, :].rearrange("p c n -> p (c n)"),
                                  AX.X, ALU.max).then_inc(max_read, 1)

            def invert(h, pair):
                eng.wait_ge(heads_moved, (h.pair0 + pair + 1) * 2 * 32)
                eng.reciprocal(inv_sums[:, pair % DT, :], sums[:, pair % DT, :]).then_inc(inverted, 1)

            def split_max(h, g):
                nth, par = h.group0 + g, g % 2
                eng.wait_ge(max_read, (nth + 1) * G * ST)
                if h.scores:
                    eng.wait_ge(ring_full, h.done("MT", g - 3) if g >= 3 else h.base)
                m1, m2 = max_parts[:, par, 0, :], max_parts[:, par, 1, :]
                eng.tensor_copy(m1, row_max[:, par, :]).then_inc(max_split, 1)
                eng.wait_ge(max_split, nth * 2 + 1)
                eng.tensor_tensor(m2, row_max[:, par, :], m1, ALU.subtract).then_inc(max_split, 1)

            def half(h):
                if h.epi is not None:
                    nth_epi = h.epi[0] * 2 + h.epi[1]
                for s in h.steps:
                    g, part = (s + LEAD) // KT, (s + LEAD) % KT
                    if s < h.maxima:
                        if part == 0:
                            at_least(eng, max_split, (h.group0 + g - 1) * 2)
                        reduce_max(h, g, 2 * part)
                        reduce_max(h, g, 2 * part + 1)
                        if part == KT - 1:
                            split_max(h, g)
                    if s in INVERT and (h.scores if INVERT[s] >= 0 else h.flush):
                        invert(h, INVERT[s])
                    if h.pro is not None:
                        if now := due(s, X_MOM):
                            if now[0] == 0:
                                eng.wait_ge(x_loaded, (h.pro + 1) * 16)
                                eng.wait_ge(x_norm, RAISED + h.pro * (KT + 1))
                            moments(x_in, st_x, KT, x_mom, h.pro, *now)
                        if h.alone:
                            between(eng, h, s)
                            if s == X_NORM:
                                part_columns()
                        if s in K_SPLIT:
                            split_k(h.pro, K_SPLIT.index(s))
                        if h.alone and s in Q_SPLIT0:
                            split_q(h.pro, 0, Q_SPLIT0.index(s))
                    if h.pro1 is not None:
                        if h.scores and s in Q_SPLIT:
                            for i in pieces(s, Q_SPLIT):
                                split_q(h.pro1, 0, i)
                        if h.scores and s in Q1_SPLIT:
                            for i in pieces(s, Q1_SPLIT):
                                split_q(h.pro1, 1, i)
                    if h.very_first and s in Q_SPLIT:
                        for i in pieces(s, Q_SPLIT):
                            split_q(0, 1, i)
                    if h.epi is not None:
                        if s == ACT_SPLIT:
                            eng.wait_ge(ring_read, h.done("HT", 1))
                            eng.tensor_copy(act_parts[:, 0, :, :], actT[:, :, :]).then_inc(act_part, 1)
                        if h.alone:
                            between(eng, h, s)
                        if now := due(s, A_MOM):
                            if now[0] == 0:
                                eng.wait_ge(a_norm, RAISED + nth_epi * (ST + 2))
                            eng.wait_ge(ring_read, h.done("WO", now[0] // 2))
                            moments(act, st_a, ST, a_mom, nth_epi, *now)
                        if now := due(s, Y_MOM):
                            if now[0] == 0:
                                eng.wait_ge(a_norm, RAISED + (nth_epi + 1) * (ST + 2))
                                eng.wait_ge(y_norm, RAISED + nth_epi * (ST + 1))
                            moments(res, st_y, ST, y_mom, nth_epi, *now)
                        if now := due(s, F_MOM):
                            if now[0] == 0:
                                eng.wait_ge(biased, (nth_epi + 1) * ST)
                                eng.wait_ge(f_norm, RAISED + nth_epi * (ST + 2))
                            moments(act, st_f, ST, f_mom, nth_epi, *now)
            schedule(half, eng, prepare)


WARM = 18
RAISED = 1
CONSTS = 8
WP_TURNED = 7


def rope_tables():
    import numpy as np
    inv = 1.0 / THETA ** (np.arange(0, D, 2, dtype=np.float32) / np.float32(D))
    ang = np.arange(S, dtype=np.float32)[None, :] * inv.astype(np.float32)[:, None]
    cs = np.stack([np.cos(ang), np.sin(ang)]).astype(np.float32)
    q = cs.reshape(2, H, NPAIR, S).transpose(0, 2, 1, 3).reshape(2, P, S)
    c, sn = (cs[i, :NPAIR].reshape(NPAIR, 2, HALF).transpose(1, 0, 2) for i in range(2))
    k = np.zeros((2, 2, NPAIR, HKV, 2, HALF), np.float32)
    k[:, :, :, :, 0] = c[:, None, :, None]
    k[:, 0, :, :, 1] = -sn[:, :, None]
    k[:, 1, :, :, 1] = sn[:, :, None]
    return np.ascontiguousarray(q), k.reshape(P, 2, HALF)


_INS = ["L0_attn_x", "L0_attn_Wq", "L0_attn_Wk", "L0_attn_Wv", "L0_attn_Wo", "L0_ffn_weight",
        "L0_ffn_alpha", "L0_ffn_bias"]


def kernel(**inputs):
    import numpy as np
    import concourse.bacc as bacc
    from concourse.bass_utils import run_bass_kernel_spmd as run

    nc = bacc.Bacc("TRN2", target_bir_lowering=False, num_devices=1)
    arrays = {f"in_{n}": np.ascontiguousarray(inputs[n]) for n in _INS}
    arrays["rope_q"], arrays["rope_k"] = rope_tables()
    args = [nc.dram_tensor(n, a.shape, F32, kind="ExternalInput").ap() for n, a in arrays.items()]
    out = nc.dram_tensor("out_0", (B, S, D), F32, kind="ExternalOutput").ap()
    sandwich_kernel(nc, *args, out)
    r = run(nc, [arrays], core_ids=[0])
    return r.results[0]["out_0"]
```
